# Optimizing a Trainium2 kernel written in Bass

```python
import numpy as np
import jax
import jax.numpy as jnp

def _softmax(x, axis=-1):
    return jax.nn.softmax(x, axis=axis)

def _gelu(x):
    return jax.nn.gelu(x, approximate=True)

def _silu(x):
    return jax.nn.silu(x)

def _sigmoid(x):
    return jax.nn.sigmoid(x)

def _layernorm(x, axis=-1, eps=1e-05):
    m = jnp.mean(x, axis=axis, keepdims=True)
    v = jnp.var(x, axis=axis, keepdims=True)
    return (x - m) / jnp.sqrt(v + eps)

def _scatter_add(tgt, idx, src, axis=0):
    return tgt.at[idx].add(src)

def _segment_sum(src, seg, n):
    return jax.ops.segment_sum(src, seg, n)
kernel_name = 'mk_adj_resnorm_d2_adj_r2_9e34f1'

def setup_inputs(seed: int=0):
    np.random.seed(seed)
    _w = jnp.asarray

    def _rec_inputs():
        import jax
        import jax.numpy as jnp
        _gk = jax.random.key(seed)
        x = -0.0005207 + 1.001 * jax.random.normal(jax.random.fold_in(_gk, 1), (4096, 256), jnp.float32)
        _w = (1.0 + jnp.arange(4096, dtype=jnp.float32)) ** (-0.5)
        _w = _w / _w.mean()
        _pij = jnp.clip(0.00195312 * _w[:, None] * _w[None, :], 0.0, 1.0)
        _a = jax.random.uniform(jax.random.fold_in(_gk, 2), (4096, 4096)) < _pij
        _af = _a.astype(jnp.float32)
        adj = _af
        return (x, adj)
    x, adj = _rec_inputs()

    def _L0_gnn_setup():
        import jax, jax.numpy as jnp
        import numpy as np
        N = 2048
        INPUT_DIM = 256
        KEY_DIM = 64
        OUT_DIM = 256
        N_HEADS = 8
        IDENTITY_BIAS = 0.01
        MASK_VAL = 1e+16

        def _xavier(key, shape, gain=np.sqrt(2.0)):
            std = gain * np.sqrt(2.0 / (shape[-2] + shape[-1]))
            return jax.random.normal(key, shape, dtype=jnp.float32) * np.float32(std)
        key = jax.random.key(seed)
        kx, ka, kk, kq, kv, ko = jax.random.split(key, 6)
        node_matrix = jax.random.normal(kx, (N, INPUT_DIM), dtype=jnp.float32)
        adjacency_matrix = jax.random.bernoulli(ka, 0.01, (N, N)).astype(jnp.float32)
        Wks = _xavier(kk, (N_HEADS, INPUT_DIM, KEY_DIM))
        Wqs = _xavier(kq, (N_HEADS, INPUT_DIM, KEY_DIM))
        Wvs = _xavier(kv, (N_HEADS, INPUT_DIM, KEY_DIM))
        Wo = _xavier(ko, (N_HEADS, KEY_DIM, OUT_DIM))
        return {'node_matrix': node_matrix, 'adjacency_matrix': adjacency_matrix, 'Wks': Wks, 'Wqs': Wqs, 'Wvs': Wvs, 'Wo': Wo}
    _L0_gnn_all = _L0_gnn_setup()
    _L0_gnn_in = {k: v for k, v in _L0_gnn_all.items() if k in ('Wks', 'Wqs', 'Wvs', 'Wo')}
    del _L0_gnn_all

    def _L1_gnn_setup():
        import jax, jax.numpy as jnp
        import numpy as np
        N = 8192
        F_IN = 256
        F_OUT = 256
        key = jax.random.key(seed)
        k = jax.random.split(key, 6)
        h = jax.random.normal(k[0], (N, F_IN), dtype=jnp.float32)
        adj = jax.random.uniform(k[1], (N, N), dtype=jnp.float32)
        W_neigh = jax.random.normal(k[2], (F_OUT, F_IN), dtype=jnp.float32) * (1.0 / np.sqrt(F_IN))
        b_neigh = jax.random.normal(k[3], (F_OUT,), dtype=jnp.float32) * 0.01
        W_self = jax.random.normal(k[4], (F_OUT, F_IN), dtype=jnp.float32) * (1.0 / np.sqrt(F_IN))
        b_self = jax.random.normal(k[5], (F_OUT,), dtype=jnp.float32) * 0.01
        return {'h': h, 'adj': adj, 'W_neigh': W_neigh, 'b_neigh': b_neigh, 'W_self': W_self, 'b_self': b_self}
    _L1_gnn_all = _L1_gnn_setup()
    _L1_gnn_in = {k: v for k, v in _L1_gnn_all.items() if k in ('W_neigh', 'b_neigh', 'W_self', 'b_self')}
    del _L1_gnn_all
    return {'x': x, 'adj': adj, 'L0_gnn_Wks': _L0_gnn_in['Wks'], 'L0_gnn_Wqs': _L0_gnn_in['Wqs'], 'L0_gnn_Wvs': _L0_gnn_in['Wvs'], 'L0_gnn_Wo': _L0_gnn_in['Wo'], 'L1_gnn_W_neigh': _L1_gnn_in['W_neigh'], 'L1_gnn_b_neigh': _L1_gnn_in['b_neigh'], 'L1_gnn_W_self': _L1_gnn_in['W_self'], 'L1_gnn_b_self': _L1_gnn_in['b_self']}

def reference(x, adj, L0_gnn_Wks, L0_gnn_Wqs, L0_gnn_Wvs, L0_gnn_Wo, L1_gnn_W_neigh, L1_gnn_b_neigh, L1_gnn_W_self, L1_gnn_b_self):
    import jax
    import jax.numpy as jnp

    def _L0_gnn_ref(node_matrix, adjacency_matrix, Wks, Wqs, Wvs, Wo):
        import jax, jax.numpy as jnp
        import numpy as np
        N = 2048
        INPUT_DIM = 256
        KEY_DIM = 64
        OUT_DIM = 256
        N_HEADS = 8
        IDENTITY_BIAS = 0.01
        MASK_VAL = 1e+16

        def _xavier(key, shape, gain=np.sqrt(2.0)):
            std = gain * np.sqrt(2.0 / (shape[-2] + shape[-1]))
            return jax.random.normal(key, shape, dtype=jnp.float32) * np.float32(std)
        n = node_matrix.shape[0]
        kd = Wks.shape[-1]
        eye = jnp.eye(n, dtype=node_matrix.dtype)
        adj = jnp.maximum(adjacency_matrix, eye)
        q = jnp.einsum('nd,hdk->hnk', node_matrix, Wqs)
        k = jnp.einsum('nd,hdk->hnk', node_matrix, Wks)
        v = jnp.einsum('nd,hdk->hnk', node_matrix, Wvs)
        scores = jnp.einsum('hqk,hmk->hqm', q, k) * kd ** (-0.5)
        scores = scores + IDENTITY_BIAS * eye - MASK_VAL * (1.0 - adj)
        att = jax.nn.softmax(scores, axis=-1)
        return jnp.einsum('hqm,hmk,hko->qo', att, v, Wo)

    def _L1_gnn_ref(h, adj, W_neigh, b_neigh, W_self, b_self):
        import jax, jax.numpy as jnp
        import numpy as np
        N = 8192
        F_IN = 256
        F_OUT = 256
        deg = jnp.sum(adj, axis=1, keepdims=True) + 1e-05
        adj_norm = adj / deg
        h_neigh = adj_norm @ h
        out = h_neigh @ W_neigh.T + b_neigh + h @ W_self.T + b_self
        return jax.nn.relu(out)
    x = _layernorm(x + _L0_gnn_ref(x, adj, L0_gnn_Wks, L0_gnn_Wqs, L0_gnn_Wvs, L0_gnn_Wo), axis=-1)
    x = _layernorm(x + _L1_gnn_ref(x, adj, L1_gnn_W_neigh, L1_gnn_b_neigh, L1_gnn_W_self, L1_gnn_b_self), axis=-1)
    return x

_drawn_inputs = setup_inputs


def setup_inputs(seed=0):
    import zlib

    import numpy as np

    out = dict(_drawn_inputs(seed))
    spreads = {}
    factors = {'L1_gnn_b_neigh': 8.0, 'L1_gnn_b_self': 8.0}
    for name, (base, spread) in spreads.items():
        noise = np.random.default_rng([zlib.crc32(name.encode()), seed]).standard_normal(out[name].shape)
        drawn = base * np.exp(spread * noise) if base else spread * noise
        out[name] = jnp.asarray(drawn.astype(out[name].dtype))
    for name, factor in factors.items():
        out[name] = (out[name] * factor).astype(out[name].dtype)
    return out
```

```python
from contextlib import ExitStack

import concourse.bass as bass
from concourse import mybir

P = 128
CHUNK = 1024
SUB = 512
LN_EPS = 1e-5
DEG_EPS = 1e-5
MASK_VAL = 1e16
IDENTITY_BIAS = 0.01
LOWEST = -3.0e38

ALU = mybir.AluOpType
ACT = mybir.ActivationFunctionType
AX = mybir.AxisListType
F32 = mybir.dt.float32
F16 = mybir.dt.float16


def gnn_two_layers(nc, x, adj, Wks, Wqs, Wvs, Wo, W_neigh, b_neigh, W_self, b_self, out):
    N, D = x.shape
    H, _, KD = Wks.shape
    T = N // P
    DC = D // P
    NC = N // CHUNK
    NS = N // SUB
    BS = SUB // P
    SCALE = float(KD) ** -0.5
    HH = H // 2
    assert 2 * KD == P and D == 2 * P and NC == 4 and NS == 8 and H == 8

    scratch = nc.dram_tensor("x_plus_attention", [N, D], F32, kind="Internal").ap()

    with ExitStack() as ctx:
        def sb(name, shape, dt):
            return ctx.enter_context(nc.sbuf_tensor(name, shape, dt))

        def sem(name):
            return ctx.enter_context(nc.semaphore(name))

        kstack = sb("kstack", [P, H, N], F16)
        vstack = sb("vstack", [P, H, T, P], F16)
        prob = sb("prob", [P, 2, N], F32)
        mask = sb("mask", [P, 2, N], F32)
        probT = sb("probT", [P, 2, BS, 2, P], F16)
        q_hi = sb("q_hi", [P, H, P], F16)
        q_lo = sb("q_lo", [P, H, P], F16)
        wq = sb("wq", [P, DC, H, KD], F32)
        wreg = sb("wreg", [P, H, D], F32)
        x_tile = sb("x_tile", [P, D], F32)
        xT_tile = sb("xT_tile", [P, DC, P], F32)
        y_tile = sb("y_tile", [P, D], F32)
        head_parts = sb("head_parts", [P, 2, P], F32)
        head_out = sb("head_out", [P, P], F32)
        diag = sb("diag", [P, P], F32)
        diag_pos = sb("diag_pos", [P, P], F32)
        ident = sb("ident", [P, P], F32)
        not_ident = sb("not_ident", [P, P], F32)
        ident16 = sb("ident16", [P, P], F16)
        chunk_max = sb("chunk_max", [P, 2, NC], F32)
        neg_max = sb("neg_max", [P, 2], F32)
        chunk_sum = sb("chunk_sum", [P, 2, NC], F32)
        row_sum = sb("row_sum", [P, 1], F32)
        inv_sum = sb("inv_sum", [P, 1], F32)
        landing, addmask = mask[:, 0, :], mask[:, 1, :]
        x_all = prob[:, :, :].rearrange("p a n -> p (a n)").rearrange("p (t d) -> p t d", d=D)
        xT_all = mask
        wflat = wreg[:, :, :].rearrange("p h d -> p (h d)")
        wk = wflat[:, 0:DC * H * KD].rearrange("p (c h k) -> p c h k", c=DC, h=H)
        wv = wflat[:, DC * H * KD:2 * DC * H * KD].rearrange("p (c h k) -> p c h k", c=DC, h=H)

        kflat = kstack[:, :, :].rearrange("p h n -> p (h n)")
        vflat = vstack[:, :, :, :].rearrange("p h t k -> p (h t k)")
        h32 = kflat[:, 0:2 * T * D].bitcast(F32).rearrange("p (t d) -> p t d", d=D)
        self_term = kflat[:, 2 * T * D:4 * T * D].bitcast(F32).rearrange("p (t d) -> p t d", d=D)
        hsplit = vflat[:, 0:2 * T * D].rearrange("p (t s d) -> p t s d", t=T, s=2)
        adj16 = [vflat[:, 2 * T * D + i * N:2 * T * D + (i + 1) * N] for i in range(2)]
        adjT = [vflat[:, 2 * T * D + (2 + i) * N:2 * T * D + (3 + i) * N] for i in range(2)]
        pflat = prob[:, :, :].rearrange("p a n -> p (a n)")

        def carve(first, *shape):
            n = 1
            for s in shape:
                n *= s
            v = pflat[:, first:first + n]
            return v if len(shape) == 1 else v.rearrange("p (a b) -> p a b", a=shape[0])

        w_raw = [carve(0, 2, D), carve(512, 2, D)]
        wT = [carve(1024, DC, D), carve(1536, DC, D)]
        bias_bc = [carve(2048, D), carve(2304, D)]
        bias_sum = carve(2560, D)
        hT = carve(2816, DC, P)
        stats = carve(3072, T, 6)
        mean_var = carve(3264, T, 2)
        std_all = carve(3328, T)
        inv_std_all = carve(3360, T)
        agg_lo = [carve(3392 + i * D, D) for i in range(2)]
        h_neigh = [carve(3904 + i * D, D) for i in range(2)]
        hnT = [carve(4416 + i * D, DC, P) for i in range(2)]
        z = [carve(4928 + i * D, D) for i in range(2)]
        o_tile = [carve(5440 + i * D, D) for i in range(2)]
        deg = [carve(5952 + i, 1) for i in range(2)]
        inv_deg = [carve(5956 + i, 1) for i in range(2)]
        stats1 = [carve(5960 + 8 * i, 6) for i in range(2)]
        mean_var1 = [carve(5976 + 2 * i, 2) for i in range(2)]
        std1 = [carve(5980 + i, 1) for i in range(2)]
        inv_std1 = [carve(5984 + i, 1) for i in range(2)]
        eps_col = carve(5988, 1)
        deg_raw = [carve(5990 + i, 1) for i in range(2)]

        banks = ctx.enter_context(nc.psum_tensor("banks", [P, 8, 512], F32))
        score_ps = [banks[:, 2 * i:2 * i + 2, :] for i in range(2)]
        trans_ps = [banks[:, 4 + i, :] for i in range(2)]
        av_ps = banks[:, 6, 0:2 * P]
        misc_ps = banks[:, 7, :]

        x_loaded, wkv_loaded, wq_loaded, wo_loaded = (
            sem("x_loaded"), sem("wkv_loaded"), sem("wq_loaded"), sem("wo_loaded"))
        xtile_loaded, adj_loaded, y_stored = sem("xtile_loaded"), sem("adj_loaded"), sem("y_stored")
        const_ready, const_step = sem("const_ready"), sem("const_step")
        xT_filled, xT_emptied = sem("xT_filled"), sem("xT_emptied")
        kv_filled, kv_hi, kv_lo = sem("kv_filled"), sem("kv_hi"), sem("kv_lo")
        scores_ready, masked_ready, neg_max_ready = (
            sem("scores_ready"), sem("masked_ready"), sem("neg_max_ready"))
        exp_ready, transposed = sem("exp_ready"), sem("transposed")
        hi_ready, lo_ready, av_done = sem("hi_ready"), sem("lo_ready"), sem("av_done")
        parts_ready, head_ready, projected, y_added = (
            sem("parts_ready"), sem("head_ready"), sem("projected"), sem("y_added"))
        sum_ready, inv_ready = sem("sum_ready"), sem("inv_ready")
        xT_made, xT_ready = sem("xT_made"), sem("xT_ready")
        q_made, q_hi_ready, q_lo_ready = sem("q_made"), sem("q_hi_ready"), sem("q_lo_ready")
        pool_step, mask_ready = sem("pool_step"), sem("mask_ready")
        y_loaded, w1_loaded = sem("y_loaded"), sem("w1_loaded")
        adj1_loaded = [sem(f"adj1_loaded_{i}") for i in range(2)]
        out_stored = [sem(f"out_stored_{i}") for i in range(2)]
        stats_ready, mv_ready, std_ready, inv_std_ready, normed = (
            sem("stats_ready"), sem("mv_ready"), sem("std_ready"), sem("inv_std_ready"), sem("normed"))
        eps_ready, bias_ready = sem("eps_ready"), sem("bias_ready")
        h_hi_ready, h_lo_ready = sem("h_hi_ready"), sem("h_lo_ready")
        wT_made, wT_ready = sem("wT_made"), sem("wT_ready")
        hT_made, hT_ready, self_made, self_ready = (
            sem("hT_made"), sem("hT_ready"), sem("self_made"), sem("self_ready"))
        adj16_ready, adjT_made, adjT_by_act, adjT_by_dve = (
            sem("adj16_ready"), sem("adjT_made"), sem("adjT_by_act"), sem("adjT_by_dve"))
        agg_done, agg_lo_ready, deg_ready, inv_deg_ready, h_neigh_ready = (
            sem("agg_done"), sem("agg_lo_ready"), sem("deg_ready"), sem("inv_deg_ready"),
            sem("h_neigh_ready"))
        hnT_made, hnT_ready, lin_done, z_step = (
            sem("hnT_made"), sem("hnT_ready"), sem("lin_done"), sem("z_step"))
        std1_ready, out_ready = sem("std1_ready"), sem("out_ready")

        adj_rows = adj.rearrange("(t p) m -> t p m", p=P)
        x_rows = x.rearrange("(t p) d -> t p d", p=P)
        scratch_rows = scratch.rearrange("(t p) d -> t p d", p=P)
        out_rows = out.rearrange("(t p) d -> t p d", p=P)

        block = ctx.enter_context(nc.Block())

        def wait_apart(eng, semaphore, value):
            eng.wait_ge(semaphore, value)
            eng.nop(nofuse=True)

        @block.sync
        def _(sp):
            sp.dma_start(x_all, x.rearrange("(t p) d -> p t d", p=P)).then_inc(x_loaded, 16)
            for c in range(DC):
                sp.dma_start(wk[:, c], Wks[:, c * P:(c + 1) * P, :].rearrange("h p k -> p h k")
                             ).then_inc(wkv_loaded, 16)
                sp.dma_start(wv[:, c], Wvs[:, c * P:(c + 1) * P, :].rearrange("h p k -> p h k")
                             ).then_inc(wkv_loaded, 16)
                sp.dma_start(wq[:, c], Wqs[:, c * P:(c + 1) * P, :].rearrange("h p k -> p h k")
                             ).then_inc(wq_loaded, 16)
            sp.dma_start(x_tile[:, :], x_rows[0]).then_inc(xtile_loaded, 16)
            sp.wait_ge(kv_filled, H * NS + T)
            sp.dma_start(landing, adj_rows[0]).then_inc(adj_loaded, 16)
            for half in range(2):
                sp.dma_start(wreg[half * KD:(half + 1) * KD], Wo.rearrange("h k o -> k h o")
                             ).then_inc(wo_loaded, 16)

            with sp.Fori(0, T - 1) as t:
                sp.wait_ge(mask_ready, t * NC + NC)
                sp.dma_start(landing, adj_rows[t + 1]).then_inc(adj_loaded, 16)
                sp.wait_ge(y_added, t * H + 1)
                sp.dma_start(x_tile[:, :], x_rows[t + 1]).then_inc(xtile_loaded, 16)
                sp.wait_ge(y_added, t * H + H)
                sp.dma_start(scratch_rows[t], y_tile[:, :]).then_inc(y_stored, 16)
            sp.wait_ge(y_added, T * H)
            sp.dma_start(scratch_rows[T - 1], y_tile[:, :]).then_inc(y_stored, 16)

            sp.wait_ge(mask_ready, T * NC)
            sp.wait_ge(masked_ready, T * H * NC)
            for i in range(2):
                sp.dma_start(mask[:, i, :], adj_rows[i]).then_inc(adj1_loaded[i], 16)
            sp.wait_ge(av_done, T * H * NS)
            sp.wait_ge(y_stored, 16 * T)
            sp.dma_start(h32, scratch.rearrange("(t p) d -> p t d", p=P)).then_inc(y_loaded, 16)
            for i, (w, b) in enumerate(((W_self, b_self), (W_neigh, b_neigh))):
                sp.dma_start(w_raw[i], w.rearrange("(c p) f -> p c f", p=P)).then_inc(w1_loaded, 16)
                sp.dma_start(bias_bc[i], b.rearrange("(a f) -> a f", a=1).broadcast_to([P, D])
                             ).then_inc(w1_loaded, 16)
            with sp.Fori(0, T // 2 - 1) as t2:
                for i in range(2):
                    sp.wait_ge(adj16_ready, 2 * t2 + i + 1)
                    sp.dma_start(mask[:, i, :], adj_rows[2 * t2 + i + 2]).then_inc(adj1_loaded[i], 16)
                for i in range(2):
                    sp.wait_ge(out_ready, 2 * t2 + i + 1)
                    sp.dma_start(out_rows[2 * t2 + i], o_tile[i]).then_inc(out_stored[i], 16)
            for i in range(2):
                sp.wait_ge(out_ready, T - 2 + i + 1)
                sp.dma_start(out_rows[T - 2 + i], o_tile[i]).then_inc(out_stored[i], 16)
            for i in range(2):
                sp.wait_ge(out_stored[i], 16 * (T // 2))

        @block.gpsimd
        def _(pool):
            pool.memset(ident[:, :], 0.0).then_inc(const_step, 1)
            pool.wait_ge(const_step, 1)
            pool.affine_select(out=ident[:, :], in_=ident[:, :], compare_op=ALU.not_equal, fill=1.0,
                               base=0, pattern=[[-1, P]], channel_multiplier=1).then_inc(const_step, 1)
            pool.wait_ge(const_step, 2)
            pool.tensor_scalar(not_ident[:, :], ident[:, :], -1.0, 1.0, ALU.mult, ALU.add
                               ).then_inc(const_ready, 1)
            pool.tensor_copy(ident16[:, :], ident[:, :]).then_inc(const_ready, 1)
            pool.wait_ge(const_ready, 2)

            POOL_STEPS = 6

            def prepare_mask(t):
                wait_apart(pool, adj_loaded, 16 * t + 16)
                base = POOL_STEPS * t
                pool.tensor_scalar(landing, landing, -1.0, None, ALU.add).then_inc(pool_step, 1)
                pool.wait_ge(pool_step, base + 1)
                here = bass.ds(t * P, P)
                pool.tensor_copy(diag[:, :], mask[:, 0, here]).then_inc(pool_step, 1)
                wait_apart(pool, pool_step, base + 2)
                pool.tensor_scalar(diag_pos[:, :], diag[:, :], 0.0, IDENTITY_BIAS / MASK_VAL,
                                   ALU.max, ALU.add).then_inc(pool_step, 1)
                pool.wait_ge(pool_step, base + 3)
                pool.tensor_tensor(diag_pos[:, :], diag_pos[:, :], ident[:, :], ALU.mult
                                   ).then_inc(pool_step, 1)
                pool.tensor_tensor(diag[:, :], diag[:, :], not_ident[:, :], ALU.mult
                                   ).then_inc(pool_step, 1)
                wait_apart(pool, pool_step, base + 5)
                pool.tensor_tensor(mask[:, 0, here], diag[:, :], diag_pos[:, :], ALU.add
                                   ).then_inc(pool_step, 1)
                pool.wait_ge(pool_step, base + 6)

            def write_mask(c):
                cols = slice(c * CHUNK, (c + 1) * CHUNK)
                pool.tensor_scalar(addmask[:, cols], landing[:, cols], MASK_VAL, None, ALU.mult
                                   ).then_inc(mask_ready, 1)

            def sum_parts(g):
                pool.wait_ge(parts_ready, g + 1)
                pool.wait_ge(projected, g)
                pool.tensor_tensor(head_out[:, :], head_parts[:, 0, :], head_parts[:, 1, :], ALU.add
                                   ).then_inc(head_ready, 1)

            prepare_mask(0)
            for c in range(NC):
                write_mask(c)

            def tile(t, last):
                for h in range(H):
                    if h == 2 and not last:
                        prepare_mask(t + 1)
                    if h == 7 and not last:
                        for c in range(NC):
                            wait_apart(pool, masked_ready, t * H * NC + 7 * NC + c + 1)
                            write_mask(c)
                    if h >= 1:
                        sum_parts(t * H + h - 1)
                sum_parts(t * H + H - 1)

            with pool.Fori(0, T - 1) as t:
                tile(t, False)
            tile(T - 1, True)

        @block.tensor
        def _(pe):
            pe.wait_ge(const_ready, 2)
            pe.wait_ge(x_loaded, 16)
            for n in range(DC * T // BS):
                if n >= 8:
                    pe.wait_ge(xT_emptied, n - 7)
                for b in range(BS):
                    blk = n * BS + b
                    mm = pe.transpose(banks[:, n % 8, b * P:(b + 1) * P],
                                      x_all[:, blk % T, (blk // T) * P:(blk // T + 1) * P], ident[:, :])
                mm.then_inc(xT_filled, 1)

            pe.wait_ge(xT_emptied, DC * T // BS)
            pe.wait_ge(wkv_loaded, 16 * 2 * DC)
            n = 0
            for h in range(H):
                for m in range(NS):
                    if n >= 8:
                        pe.wait_ge(kv_lo, n - 7)
                    for half in range(2):
                        for c in range(DC):
                            mm = pe.matmul(banks[half * KD:(half + 1) * KD, n % 8, :], wk[:, c, h, :],
                                           xT_all[:, c, m * SUB:(m + 1) * SUB],
                                           start=(c == 0), stop=(c == DC - 1))
                    mm.then_inc(kv_filled, 1)
                    n += 1
            for t in range(T):
                pe.wait_ge(kv_lo, n - 7)
                for c in range(DC):
                    mm = pe.matmul(banks[:, n % 8, :], xT_all[:, c, t * P:(t + 1) * P],
                                   wv[:, c].rearrange("p h k -> p (h k)"),
                                   start=(c == 0), stop=(c == DC - 1))
                mm.then_inc(kv_filled, 1)
                n += 1
            pe.wait_ge(kv_lo, n)
            pe.wait_ge(wq_loaded, 16 * DC)
            pe.wait_ge(wo_loaded, 32)

            def make_xT(t):
                pe.wait_ge(xtile_loaded, 16 * t + 16)
                for c in range(DC):
                    mm = pe.transpose(misc_ps[:, c * P:(c + 1) * P], x_tile[:, c * P:(c + 1) * P],
                                      ident[:, :])
                mm.then_inc(xT_made, 1)

            def make_q(t, part):
                pe.wait_ge(xT_ready, t + 1)
                for j in range(HH):
                    for half in range(2):
                        for c in range(DC):
                            mm = pe.matmul(misc_ps[half * KD:(half + 1) * KD, j * P:(j + 1) * P],
                                           wq[:, c, part * HH + j, :], xT_tile[:, c, :],
                                           start=(c == 0), stop=(c == DC - 1), skip_group_check=True)
                mm.then_inc(q_made, 1)

            def scores(g, h, c, t):
                if c == 0 and h % HH == 0:
                    pe.wait_ge(q_lo_ready, 2 * t + h // HH + 1)
                if not (isinstance(g, int) and g == 0 and c < 2):
                    pe.wait_ge(masked_ready, g * NC + c - 1)
                for part, q in enumerate((q_hi, q_lo)):
                    for b in range(CHUNK // SUB):
                        mm = pe.matmul(score_ps[c % 2][:, b, :], q[:, h, :],
                                       kstack[:, h, c * CHUNK + b * SUB:c * CHUNK + (b + 1) * SUB],
                                       start=(part == 0), stop=(part == 1), skip_group_check=True)
                mm.then_inc(scores_ready, 1)

            def turn(g, h, s):
                if s % 2 == 0:
                    pe.wait_ge(exp_ready, g * NC + s // 2 + 1)
                for b in range(BS):
                    m = s * BS + b
                    mm = pe.transpose(trans_ps[s % 2][:, b * P:(b + 1) * P],
                                      prob[:, h % 2, m * P:(m + 1) * P], ident[:, :])
                mm.then_inc(transposed, 1)

            def values(g, h, s):
                pe.wait_ge(lo_ready, g * NS + s + 1)
                if s == 0 and h > 0:
                    pe.wait_ge(parts_ready, g)
                for b in range(BS):
                    m = s * BS + b
                    mm = pe.matmul(av_ps, vstack[:, h, m, :],
                                   probT[:, s % 2, b].rearrange("p s q -> p (s q)"),
                                   start=(m == 0), stop=(m == T - 1))
                mm.then_inc(av_done, 1)

            def project(g, h):
                pe.wait_ge(head_ready, g + 1)
                mm = pe.matmul(misc_ps[:, 0:D], head_out[:, :], wreg[:, h, :], start=True, stop=True)
                mm.then_inc(projected, 1)

            make_xT(0)
            make_q(0, 0)
            pe.wait_ge(q_lo_ready, 1)
            make_q(0, 1)
            for c in range(NC):
                scores(0, 0, c, 0)

            def tile(t, last):
                for h in range(H):
                    g = t * H + h
                    ahead = not (last and h == H - 1)
                    nh, nt = (h + 1, t) if h < H - 1 else (0, t + 1)
                    if ahead:
                        scores(g + 1, nh, 0, nt)
                    turn(g, h, 0)
                    if h > 0:
                        values(g - 1, h - 1, NS - 1)
                    if ahead:
                        scores(g + 1, nh, 1, nt)
                    turn(g, h, 1)
                    if ahead:
                        scores(g + 1, nh, 2, nt)
                    values(g, h, 0)
                    turn(g, h, 2)
                    values(g, h, 1)
                    turn(g, h, 3)
                    if ahead:
                        scores(g + 1, nh, 3, nt)
                    values(g, h, 2)
                    turn(g, h, 4)
                    if h > 0:
                        project(g - 1, h - 1)
                    values(g, h, 3)
                    turn(g, h, 5)
                    if h == 3 and not last:
                        pe.wait_ge(y_added, g)
                        make_xT(t + 1)
                    if h == 4 and not last:
                        pe.wait_ge(y_added, g)
                        make_q(t + 1, 0)
                    if h == 7 and not last:
                        pe.wait_ge(y_added, g)
                        make_q(t + 1, 1)
                    values(g, h, 4)
                    turn(g, h, 6)
                    values(g, h, 5)
                    turn(g, h, 7)
                    values(g, h, 6)
                    if h == 4 and not last:
                        pe.wait_ge(q_lo_ready, 2 * t + 3)
                    if h == 3 and not last:
                        pe.wait_ge(xT_ready, t + 2)
                values(t * H + H - 1, H - 1, NS - 1)
                if not last:
                    pe.wait_ge(q_lo_ready, 2 * t + 4)
                project(t * H + H - 1, H - 1)

            with pe.Fori(0, T - 1) as t:
                tile(t, False)
            tile(T - 1, True)

            pe.wait_ge(y_added, T * H)
            pe.wait_ge(w1_loaded, 64)
            for i in range(2):
                for c in range(DC):
                    for o in range(2):
                        mm = pe.transpose(banks[:, i, c * D + o * P:c * D + (o + 1) * P],
                                          w_raw[i][:, o, c * P:(c + 1) * P], ident[:, :])
                mm.then_inc(wT_made, 1)
            pe.wait_ge(wT_ready, 2)
            for t in range(T):
                pe.wait_ge(normed, t + 1)
                if t >= 1:
                    pe.wait_ge(hT_ready, t)
                for c in range(DC):
                    mm = pe.transpose(banks[:, 2, c * P:(c + 1) * P], h32[:, t, c * P:(c + 1) * P],
                                      ident[:, :])
                mm.then_inc(hT_made, 1)
                pe.wait_ge(hT_ready, t + 1)
                if t >= 1:
                    pe.wait_ge(self_ready, t)
                for c in range(DC):
                    mm = pe.matmul(banks[:, 3, 0:D], hT[:, c, :], wT[0][:, c, :],
                                   start=(c == 0), stop=(c == DC - 1))
                mm.then_inc(self_made, 1)

            def turn_adj(t, i, k):
                if k == 0:
                    pe.wait_ge(adj16_ready, t + 1)
                if not (isinstance(t, int) and t == 0):
                    pe.wait_ge(adjT_by_act if k % 2 == 0 else adjT_by_dve, 2 * t + k // 2 - 1)
                bank = banks[:, k, :].bitcast(F16)
                for b in range(8):
                    m = 8 * k + b
                    mm = pe.transpose(bank[:, b * P:(b + 1) * P], adj16[i][:, m * P:(m + 1) * P],
                                      ident16[:, :])
                mm.then_inc(adjT_made, 1)

            def aggregate(t, i, k):
                pe.wait_ge(adjT_by_act if k % 2 == 0 else adjT_by_dve, 2 * t + k // 2 + 1)
                for b in range(8):
                    m = 8 * k + b
                    mm = pe.matmul(banks[:, 4 + i, :], adjT[i][:, m * P:(m + 1) * P],
                                   hsplit[:, m].rearrange("p s d -> p (s d)"),
                                   start=(m == 0), stop=(m == T - 1))
                if k == 3:
                    mm.then_inc(agg_done, 1)

            def turn_neigh(t, i):
                pe.wait_ge(h_neigh_ready, t + 1)
                for c in range(DC):
                    mm = pe.transpose(banks[:, 6, c * P:(c + 1) * P], h_neigh[i][:, c * P:(c + 1) * P],
                                      ident[:, :])
                mm.then_inc(hnT_made, 1)

            def linear(t, i):
                pe.wait_ge(hnT_ready, t + 1)
                for c in range(DC):
                    mm = pe.matmul(banks[:, 7, 0:D], hnT[i][:, c, :], wT[1][:, c, :],
                                   start=(c == 0), stop=(c == DC - 1))
                mm.then_inc(lin_done, 1)

            pe.wait_ge(self_ready, T)
            pe.wait_ge(h_lo_ready, T)
            for k in range(4):
                turn_adj(0, 0, k)

            def pair(t2, last):
                for i in range(2):
                    t = 2 * t2 + i
                    for k in range(4):
                        if not (last and i == 1):
                            turn_adj(t + 1, 1 - i, k)
                        aggregate(t, i, k)
                    turn_neigh(t, i)
                    linear(t, i)

            with pe.Fori(0, T // 2 - 1) as t2:
                pair(t2, False)
            pair(T // 2 - 1, True)

        @block.scalar
        def _(act):
            for n in range(DC * T // BS):
                act.wait_ge(xT_filled, n + 1)
                blk = n * BS
                act.activation(xT_all[:, blk // T, (blk % T) * P:(blk % T + BS) * P], banks[:, n % 8, :],
                               ACT.Copy).then_inc(xT_emptied, 1)
            n = 0
            for h in range(H):
                for m in range(NS):
                    act.wait_ge(kv_filled, n + 1)
                    act.activation(kstack[:, h, m * SUB:(m + 1) * SUB], banks[:, n % 8, :], ACT.Copy
                                   ).then_inc(kv_hi, 1)
                    n += 1
            for t in range(T):
                act.wait_ge(kv_filled, n + 1)
                act.activation(vstack[:, :, t, 0:KD], banks[:, n % 8, :].rearrange("p (h k) -> p h k", h=H),
                               ACT.Copy).then_inc(kv_hi, 1)
                n += 1

            def copy_xT(t):
                act.wait_ge(xT_made, t + 1)
                act.activation(xT_tile[:, :, :].rearrange("p c q -> p (c q)"), misc_ps[:, 0:D], ACT.Copy
                               ).then_inc(xT_ready, 1)

            def high_q(t, part):
                act.wait_ge(q_made, 2 * t + part + 1)
                act.activation(q_hi[:, part * HH:(part + 1) * HH, :].rearrange("p h q -> p (h q)"), misc_ps,
                               ACT.Copy, scale=SCALE).then_inc(q_hi_ready, 1)

            def exps(g, h, c):
                if c == 0:
                    act.wait_ge(neg_max_ready, g + 1)
                cols = prob[:, h % 2, c * CHUNK:(c + 1) * CHUNK]
                act.activation(cols, cols, ACT.Exp, bias=neg_max[:, h % 2:h % 2 + 1],
                               accum_out=chunk_sum[:, h % 2, c:c + 1]).then_inc(exp_ready, 1)

            def high(g, s):
                act.wait_ge(transposed, g * NS + s + 1)
                act.activation(probT[:, s % 2, :, 0, :], trans_ps[s % 2].rearrange("p (b q) -> p b q", b=BS),
                               ACT.Copy).then_inc(hi_ready, 1)

            def take_parts(g, first):
                act.wait_ge(av_done, g * NS + NS)
                if not first:
                    act.wait_ge(head_ready, g)
                act.activation(head_parts[:, :, :].rearrange("p s q -> p (s q)"), av_ps, ACT.Copy
                               ).then_inc(parts_ready, 1)

            copy_xT(0)
            high_q(0, 0)
            high_q(0, 1)
            exps(0, 0, 0)

            def tile(t, last):
                for h in range(H):
                    g = t * H + h
                    exps(g, h, 1)
                    high(g, 0)
                    if h > 0:
                        take_parts(g - 1, False)
                    high(g, 1)
                    exps(g, h, 2)
                    high(g, 2)
                    high(g, 3)
                    exps(g, h, 3)
                    high(g, 4)
                    high(g, 5)
                    if h == 3 and not last:
                        copy_xT(t + 1)
                    if h == 4 and not last:
                        high_q(t + 1, 0)
                    if h == 7 and not last:
                        high_q(t + 1, 1)
                    if not (last and h == H - 1):
                        exps(g + 1, h + 1, 0)
                    high(g, 6)
                    high(g, 7)
                take_parts(t * H + H - 1, False)

            with act.Fori(0, T - 1) as t:
                tile(t, False)
            tile(T - 1, True)

            for i in range(2):
                act.wait_ge(wT_made, i + 1)
                act.activation(wT[i].rearrange("p c o -> p (c o)"), banks[:, i, :], ACT.Copy
                               ).then_inc(wT_ready, 1)
            act.wait_ge(eps_ready, 1)
            act.wait_ge(mv_ready, T)
            act.activation(std_all, mean_var[:, :, 1], ACT.Sqrt, bias=eps_col).then_inc(std_ready, 1)
            for t in range(T):
                act.wait_ge(normed, t + 1)
                act.activation(hsplit[:, t, 0, :], h32[:, t, :], ACT.Copy).then_inc(h_hi_ready, 1)
                act.wait_ge(hT_made, t + 1)
                if t >= 1:
                    act.wait_ge(self_made, t)
                act.activation(hT.rearrange("p c q -> p (c q)"), banks[:, 2, 0:D], ACT.Copy
                               ).then_inc(hT_ready, 1)

            def convert(t, i, t2):
                act.wait_ge(adj1_loaded[i], 16 * t2 + 16)
                if not (isinstance(t, int) and t < 2):
                    act.wait_ge(adjT_made, 4 * t - 4)
                    act.wait_ge(inv_deg_ready, 2 * t - 2)
                act.activation(adj16[i], mask[:, i, :], ACT.Copy, accum_out=deg_raw[i]
                               ).then_inc(adj16_ready, 1)

            def empty_adj(t, i, k):
                act.wait_ge(adjT_made, 4 * t + k + 1)
                if not (isinstance(t, int) and t < 2):
                    act.wait_ge(agg_done, t - 1)
                act.activation(adjT[i][:, 8 * k * P:8 * (k + 1) * P], banks[:, k, :].bitcast(F16), ACT.Copy
                               ).then_inc(adjT_by_act, 1)

            def finish(t, i):
                act.wait_ge(agg_done, t + 1)
                act.wait_ge(inv_deg_ready, 2 * t + 2)
                act.activation(agg_lo[i], banks[:, 4 + i, D:2 * D], ACT.Copy, scale=inv_deg[i]
                               ).then_inc(agg_lo_ready, 1)
                act.wait_ge(hnT_made, t + 1)
                act.activation(hnT[i].rearrange("p c q -> p (c q)"), banks[:, 6, 0:D], ACT.Copy
                               ).then_inc(hnT_ready, 1)
                act.wait_ge(z_step, 4 * t + 4)
                act.activation(std1[i], mean_var1[i][:, 1:2], ACT.Sqrt, bias=eps_col).then_inc(std1_ready, 1)

            act.wait_ge(h_lo_ready, T)
            convert(0, 0, 0)
            empty_adj(0, 0, 0)
            empty_adj(0, 0, 2)
            convert(1, 1, 0)

            def pair(t2, last):
                for i in range(2):
                    t = 2 * t2 + i
                    if not (last and i == 1):
                        empty_adj(t + 1, 1 - i, 0)
                        empty_adj(t + 1, 1 - i, 2)
                    if not last:
                        convert(t + 2, i, t2 + 1)
                    finish(t, i)

            with act.Fori(0, T // 2 - 1) as t2:
                pair(t2, False)
            pair(T // 2 - 1, True)

        @block.vector
        def _(dve):
            n = 0
            for h in range(H):
                for m in range(NS):
                    dve.wait_ge(kv_hi, n + 1)
                    low = kstack[KD:P, h, m * SUB:(m + 1) * SUB]
                    dve.tensor_tensor(low, banks[KD:P, n % 8, :], low, ALU.subtract).then_inc(kv_lo, 1)
                    n += 1
            for t in range(T):
                dve.wait_ge(kv_hi, n + 1)
                dve.tensor_tensor(vstack[:, :, t, KD:P], banks[:, n % 8, :].rearrange("p (h k) -> p h k", h=H),
                                  vstack[:, :, t, 0:KD], ALU.subtract).then_inc(kv_lo, 1)
                n += 1

            def low_q(t, part):
                dve.wait_ge(q_hi_ready, 2 * t + part + 1)
                heads = slice(part * HH, (part + 1) * HH)
                dve.scalar_tensor_tensor(out=q_lo[:, heads, :].rearrange("p h q -> p (h q)"), in0=misc_ps,
                                         scalar=SCALE, in1=q_hi[:, heads, :].rearrange("p h q -> p (h q)"),
                                         op0=ALU.mult, op1=ALU.subtract).then_inc(q_lo_ready, 1)

            def add_mask(g, h, c, t):
                if h == 0:
                    wait_apart(dve, mask_ready, t * NC + c + 1)
                wait_apart(dve, scores_ready, g * NC + c + 1)
                cols = slice(c * CHUNK, (c + 1) * CHUNK)
                dve.tensor_tensor_reduce(prob[:, h % 2, cols],
                                         score_ps[c % 2].rearrange("p b n -> p (b n)"), addmask[:, cols],
                                         1.0, LOWEST, ALU.add, ALU.max,
                                         chunk_max[:, h % 2, c:c + 1]).then_inc(masked_ready, 1)

            def max_of_row(g, h):
                dve.wait_ge(masked_ready, g * NC + NC)
                dve.tensor_reduce(neg_max[:, h % 2:h % 2 + 1], chunk_max[:, h % 2, :], AX.X, ALU.max,
                                  negate=True).then_inc(neg_max_ready, 1)

            def low(g, s):
                dve.wait_ge(hi_ready, g * NS + s + 1)
                dve.tensor_tensor(probT[:, s % 2, :, 1, :], trans_ps[s % 2].rearrange("p (b q) -> p b q", b=BS),
                                  probT[:, s % 2, :, 0, :], ALU.subtract).then_inc(lo_ready, 1)

            def invert_sum(g, h):
                dve.wait_ge(exp_ready, g * NC + NC)
                dve.tensor_reduce(row_sum[:, :], chunk_sum[:, h % 2, :], AX.X, ALU.add).then_inc(sum_ready, 1)
                dve.wait_ge(sum_ready, g + 1)
                dve.reciprocal(inv_sum[:, :], row_sum[:, :]).then_inc(inv_ready, 1)

            def add_head(g, h, t):
                dve.wait_ge(projected, g + 1)
                dve.wait_ge(inv_ready, g + 1)
                if h == 0:
                    dve.wait_ge(y_stored, 16 * t)
                    dve.wait_ge(xtile_loaded, 16 * t + 16)
                else:
                    dve.wait_ge(y_added, g)
                dve.scalar_tensor_tensor(out=y_tile[:, :], in0=misc_ps[:, 0:D], scalar=inv_sum[:, 0:1],
                                         in1=x_tile[:, :] if h == 0 else y_tile[:, :],
                                         op0=ALU.mult, op1=ALU.add).then_inc(y_added, 1)

            low_q(0, 0)
            low_q(0, 1)
            for c in range(NC):
                add_mask(0, 0, c, 0)
            max_of_row(0, 0)

            def tile(t, last):
                for h in range(H):
                    g = t * H + h
                    ahead = not (last and h == H - 1)
                    nh, nt = (h + 1, t) if h < H - 1 else (0, t + 1)
                    if ahead:
                        add_mask(g + 1, nh, 0, nt)
                        add_mask(g + 1, nh, 1, nt)
                    low(g, 0)
                    low(g, 1)
                    low(g, 2)
                    if ahead:
                        add_mask(g + 1, nh, 2, nt)
                    low(g, 3)
                    if h > 0:
                        add_head(g - 1, h - 1, t)
                    low(g, 4)
                    if ahead:
                        add_mask(g + 1, nh, 3, nt)
                        max_of_row(g + 1, nh)
                    low(g, 5)
                    if h == 4 and not last:
                        low_q(t + 1, 0)
                    if h == 7 and not last:
                        low_q(t + 1, 1)
                    low(g, 6)
                    low(g, 7)
                    invert_sum(g, h)
                add_head(t * H + H - 1, H - 1, t)

            with dve.Fori(0, T - 1) as t:
                tile(t, False)
            tile(T - 1, True)

            dve.memset(eps_col, LN_EPS).then_inc(eps_ready, 1)
            dve.wait_ge(w1_loaded, 64)
            dve.tensor_tensor(bias_sum, bias_bc[0], bias_bc[1], ALU.add).then_inc(bias_ready, 1)
            dve.wait_ge(y_loaded, 16)
            for t in range(T):
                dve.bn_stats(stats[:, t, :], h32[:, t, :]).then_inc(stats_ready, 1)
                dve.wait_ge(stats_ready, t + 1)
                dve.bn_aggr(mean_var[:, t, :], stats[:, t, :]).then_inc(mv_ready, 1)
            dve.wait_ge(std_ready, 1)
            dve.reciprocal(inv_std_all, std_all).then_inc(inv_std_ready, 1)
            dve.wait_ge(inv_std_ready, 1)
            dve.wait_ge(mv_ready, T)
            for t in range(T):
                dve.tensor_scalar(h32[:, t, :], h32[:, t, :], mean_var[:, t, 0:1], inv_std_all[:, t:t + 1],
                                  ALU.subtract, ALU.mult).then_inc(normed, 1)
            dve.wait_ge(bias_ready, 1)
            for t in range(T):
                dve.wait_ge(h_hi_ready, t + 1)
                dve.tensor_tensor(hsplit[:, t, 1, :], h32[:, t, :], hsplit[:, t, 0, :], ALU.subtract
                                  ).then_inc(h_lo_ready, 1)
                dve.wait_ge(self_made, t + 1)
                dve.tensor_tensor(self_term[:, t, :], banks[:, 3, 0:D], bias_sum, ALU.add
                                  ).then_inc(self_ready, 1)

            def degree(t, i):
                dve.wait_ge(adj16_ready, t + 1)
                if not (isinstance(t, int) and t < 2):
                    dve.wait_ge(h_neigh_ready, t - 1)
                dve.tensor_scalar(deg[i], deg_raw[i], DEG_EPS, None, ALU.add).then_inc(inv_deg_ready, 1)
                dve.wait_ge(inv_deg_ready, 2 * t + 1)
                dve.reciprocal(inv_deg[i], deg[i]).then_inc(inv_deg_ready, 1)

            def empty_adj(t, i, k):
                dve.wait_ge(adjT_made, 4 * t + k + 1)
                if not (isinstance(t, int) and t < 2):
                    dve.wait_ge(agg_done, t - 1)
                dve.tensor_copy(adjT[i][:, 8 * k * P:8 * (k + 1) * P], banks[:, k, :].bitcast(F16)
                                ).then_inc(adjT_by_dve, 1)

            def finish(t, i, t2):
                dve.wait_ge(agg_lo_ready, t + 1)
                dve.scalar_tensor_tensor(out=h_neigh[i], in0=banks[:, 4 + i, 0:D], scalar=inv_deg[i],
                                         in1=agg_lo[i], op0=ALU.mult, op1=ALU.add).then_inc(h_neigh_ready, 1)
                dve.wait_ge(lin_done, t + 1)
                dve.tensor_tensor(z[i], banks[:, 7, 0:D], self_term[:, t, :], ALU.add).then_inc(z_step, 1)
                dve.wait_ge(z_step, 4 * t + 1)
                dve.scalar_tensor_tensor(out=z[i], in0=z[i], scalar=0.0, in1=h32[:, t, :],
                                         op0=ALU.max, op1=ALU.add).then_inc(z_step, 1)
                dve.wait_ge(z_step, 4 * t + 2)
                dve.bn_stats(stats1[i], z[i]).then_inc(z_step, 1)
                wait_apart(dve, z_step, 4 * t + 3)
                dve.bn_aggr(mean_var1[i], stats1[i]).then_inc(z_step, 1)
                dve.wait_ge(std1_ready, t + 1)
                dve.reciprocal(inv_std1[i], std1[i]).then_inc(inv_std_ready, 1)
                dve.wait_ge(inv_std_ready, t + 2)
                dve.wait_ge(out_stored[i], 16 * t2)
                dve.tensor_scalar(o_tile[i], z[i], mean_var1[i][:, 0:1], inv_std1[i],
                                  ALU.subtract, ALU.mult).then_inc(out_ready, 1)

            degree(0, 0)
            empty_adj(0, 0, 1)
            empty_adj(0, 0, 3)

            def pair(t2, last):
                for i in range(2):
                    t = 2 * t2 + i
                    if not (last and i == 1):
                        degree(t + 1, 1 - i)
                        empty_adj(t + 1, 1 - i, 1)
                        empty_adj(t + 1, 1 - i, 3)
                    finish(t, i, t2)

            with dve.Fori(0, T // 2 - 1) as t2:
                pair(t2, False)
            pair(T // 2 - 1, True)


_INS = ['x', 'adj', 'L0_gnn_Wks', 'L0_gnn_Wqs', 'L0_gnn_Wvs', 'L0_gnn_Wo',
        'L1_gnn_W_neigh', 'L1_gnn_b_neigh', 'L1_gnn_W_self', 'L1_gnn_b_self']
_OUTS = [((4096, 256), 'float32')]


def kernel(**inputs):
    import numpy as _np
    import concourse.bacc as _bacc
    from concourse import mybir as _mybir
    from concourse.bass_utils import run_bass_kernel_spmd as _run

    nc = _bacc.Bacc("TRN2", target_bir_lowering=False, num_devices=1, dynamic_dma_scratch_size=1024)
    arrays, args = {}, []
    for name in _INS:
        a = _np.ascontiguousarray(inputs[name])
        arrays[f"in_{name}_dram"] = a
        args.append(nc.dram_tensor(f"in_{name}_dram", a.shape, _mybir.dt.from_np(a.dtype), kind="ExternalInput").ap())
    for i, (shape, dtype) in enumerate(_OUTS):
        dt = _mybir.dt.from_np(_np.dtype(dtype))
        args.append(nc.dram_tensor(f"out_{i}_dram", shape, dt, kind="ExternalOutput").ap())
    gnn_two_layers(nc, *args)
    r = _run(nc, [arrays], core_ids=[0])
    got = tuple(r.results[0][f"out_{i}_dram"] for i in range(len(_OUTS)))
    return got[0]
```

```python
from contextlib import ExitStack

import concourse.bass as bass
from concourse import mybir

P = 128
CHUNK = 1024
SUB = 512
LN_EPS = 1e-5
DEG_EPS = 1e-5
MASK_VAL = 1e16
IDENTITY_BIAS = 0.01
LOWEST = -3.0e38

ALU = mybir.AluOpType
ACT = mybir.ActivationFunctionType
AX = mybir.AxisListType
F32 = mybir.dt.float32
F16 = mybir.dt.float16


def gnn_two_layers(nc, x, adj, Wks, Wqs, Wvs, Wo, W_neigh, b_neigh, W_self, b_self, out):
    N, D = x.shape
    H, _, KD = Wks.shape
    T = N // P
    DC = D // P
    NC = N // CHUNK
    NS = N // SUB
    BS = SUB // P
    SCALE = float(KD) ** -0.5
    HH = H // 2
    NPT = 4
    Q_HEADS = (3, 4, 7)
    assert 2 * KD == P and D == 2 * P and NC == 4 and NS == 8 and H == 8

    scratch = nc.dram_tensor("x_plus_attention", [N, D], F32, kind="Internal").ap()

    with ExitStack() as ctx:
        def sb(name, shape, dt):
            return ctx.enter_context(nc.sbuf_tensor(name, shape, dt))

        def sem(name):
            return ctx.enter_context(nc.semaphore(name))

        kstack = sb("kstack", [P, H, N], F16)
        vstack = sb("vstack", [P, H, T, P], F16)
        prob = sb("prob", [P, 2, N], F32)
        mask = sb("mask", [P, 2, N], F32)
        probT = sb("probT", [P, NPT, BS, 2, P], F16)
        q_hi = sb("q_hi", [P, H, P], F16)
        q_lo = sb("q_lo", [P, H, P], F16)
        wq = sb("wq", [P, DC, H, KD], F32)
        wreg = sb("wreg", [P, H, D], F32)
        x_tile = sb("x_tile", [P, D], F32)
        xT_tile = sb("xT_tile", [P, DC, P], F32)
        y_tile = sb("y_tile", [P, D], F32)
        head_parts = sb("head_parts", [P, 2, P], F32)
        head_out = sb("head_out", [P, P], F32)
        diag = sb("diag", [P, P], F32)
        diag_pos = sb("diag_pos", [P, P], F32)
        ident = sb("ident", [P, P], F32)
        not_ident = sb("not_ident", [P, P], F32)
        chunk_max = sb("chunk_max", [P, 2, NC], F32)
        neg_max = sb("neg_max", [P, 2], F32)
        chunk_sum = sb("chunk_sum", [P, 2, NC], F32)
        row_sum = sb("row_sum", [P, 1], F32)
        inv_sum = sb("inv_sum", [P, 1], F32)
        landing, addmask = mask[:, 0, :], mask[:, 1, :]
        x_all = prob[:, :, :].rearrange("p a n -> p (a n)").rearrange("p (t d) -> p t d", d=D)
        xT_all = mask
        wflat = wreg[:, :, :].rearrange("p h d -> p (h d)")
        wk = wflat[:, 0:DC * H * KD].rearrange("p (c h k) -> p c h k", c=DC, h=H)
        wv = wflat[:, DC * H * KD:2 * DC * H * KD].rearrange("p (c h k) -> p c h k", c=DC, h=H)

        kflat = kstack[:, :, :].rearrange("p h n -> p (h n)")
        vflat = vstack[:, :, :, :].rearrange("p h t k -> p (h t k)")
        h32 = kflat[:, 0:2 * T * D].bitcast(F32).rearrange("p (t d) -> p t d", d=D)
        self_term = kflat[:, 2 * T * D:4 * T * D].bitcast(F32).rearrange("p (t d) -> p t d", d=D)
        hsplit = vflat[:, 0:2 * T * D].rearrange("p (t s d) -> p t s d", t=T, s=2)
        adj16 = [vflat[:, 2 * T * D + i * N:2 * T * D + (i + 1) * N] for i in range(2)]
        adjT = [vflat[:, 2 * T * D + (2 + i) * N:2 * T * D + (3 + i) * N] for i in range(2)]
        pflat = prob[:, :, :].rearrange("p a n -> p (a n)")

        def carve(first, *shape):
            n = 1
            for s in shape:
                n *= s
            v = pflat[:, first:first + n]
            return v if len(shape) == 1 else v.rearrange("p (a b) -> p a b", a=shape[0])

        w_raw = [carve(0, 2, D), carve(512, 2, D)]
        wT = [carve(1024, DC, D), carve(1536, DC, D)]
        bias_bc = [carve(2048, D), carve(2304, D)]
        bias_sum = carve(2560, D)
        hT = carve(2816, DC, P)
        stats = carve(3072, T, 6)
        mean_var = carve(3264, T, 2)
        std_all = carve(3328, T)
        inv_std_all = carve(3360, T)
        agg_lo = [carve(3392 + i * D, D) for i in range(2)]
        h_neigh = [carve(3904 + i * D, D) for i in range(2)]
        hnT = [carve(4416 + i * D, DC, P) for i in range(2)]
        z = [carve(4928 + i * D, D) for i in range(2)]
        o_tile = [carve(5440 + i * D, D) for i in range(2)]
        deg = [carve(5952 + i, 1) for i in range(2)]
        inv_deg = [carve(5956 + i, 1) for i in range(2)]
        stats1 = [carve(5960 + 8 * i, 6) for i in range(2)]
        mean_var1 = [carve(5976 + 2 * i, 2) for i in range(2)]
        std1 = [carve(5980 + i, 1) for i in range(2)]
        inv_std1 = [carve(5984 + i, 1) for i in range(2)]
        eps_col = carve(5988, 1)
        deg_raw = [carve(5990 + i, 1) for i in range(2)]
        ident16 = carve(6016, P // 2).bitcast(F16)

        banks = ctx.enter_context(nc.psum_tensor("banks", [P, 8, 512], F32))
        score_ps = [banks[:, 2 * i:2 * i + 2, :] for i in range(2)]
        turn_ps = [banks[:, 4 + i, :] for i in range(3)]
        av_ps = banks[:, 7, 0:2 * P]

        def bank_of(h, use):
            before = sum(q < h for q in Q_HEADS)
            late = int(h in Q_HEADS)
            place = {"project": 4, "queries": 7}.get(use)
            if place is None:
                place = use if use < 4 else use + 1 if use < 6 else use + 1 + late
            return turn_ps[((NS + 1) * h + before + place) % 3]
        assert (H * (NS + 1) + len(Q_HEADS)) % 3 == 0

        x_loaded, wkv_loaded, wq_loaded, wo_loaded = (
            sem("x_loaded"), sem("wkv_loaded"), sem("wq_loaded"), sem("wo_loaded"))
        xtile_loaded, adj_loaded, y_stored = sem("xtile_loaded"), sem("adj_loaded"), sem("y_stored")
        const_ready, const_step = sem("const_ready"), sem("const_step")
        xT_filled, xT_emptied = sem("xT_filled"), sem("xT_emptied")
        kv_filled, kv_hi, kv_lo = sem("kv_filled"), sem("kv_hi"), sem("kv_lo")
        scores_ready, masked_ready, neg_max_ready = (
            sem("scores_ready"), sem("masked_ready"), sem("neg_max_ready"))
        exp_ready, transposed = sem("exp_ready"), sem("transposed")
        hi_ready, lo_ready, av_done = sem("hi_ready"), sem("lo_ready"), sem("av_done")
        parts_ready, head_ready, projected, y_added = (
            sem("parts_ready"), sem("head_ready"), sem("projected"), sem("y_added"))
        sum_ready, inv_ready = sem("sum_ready"), sem("inv_ready")
        xT_made, xT_ready = sem("xT_made"), sem("xT_ready")
        q_made, q_hi_ready, q_lo_ready = sem("q_made"), sem("q_hi_ready"), sem("q_lo_ready")
        pool_step, mask_ready = sem("pool_step"), sem("mask_ready")
        y_loaded, y_last_loaded, w1_loaded = sem("y_loaded"), sem("y_last_loaded"), sem("w1_loaded")
        adj1_loaded = [sem(f"adj1_loaded_{i}") for i in range(2)]
        out_stored = [sem(f"out_stored_{i}") for i in range(2)]
        stats_ready, mv_ready, std_ready, inv_std_ready, normed = (
            sem("stats_ready"), sem("mv_ready"), sem("std_ready"), sem("inv_std_ready"), sem("normed"))
        eps_ready, bias_ready, ident16_ready = sem("eps_ready"), sem("bias_ready"), sem("ident16_ready")
        h_hi_ready, h_lo_ready = sem("h_hi_ready"), sem("h_lo_ready")
        wT_made, wT_ready = sem("wT_made"), sem("wT_ready")
        hT_made, hT_ready, self_made, self_ready = (
            sem("hT_made"), sem("hT_ready"), sem("self_made"), sem("self_ready"))
        adj16_ready, adjT_made, adjT_by_act, adjT_by_dve = (
            sem("adj16_ready"), sem("adjT_made"), sem("adjT_by_act"), sem("adjT_by_dve"))
        agg_done, agg_lo_ready, deg_ready, inv_deg_ready, h_neigh_ready = (
            sem("agg_done"), sem("agg_lo_ready"), sem("deg_ready"), sem("inv_deg_ready"),
            sem("h_neigh_ready"))
        hnT_made, hnT_ready, lin_done, z_step = (
            sem("hnT_made"), sem("hnT_ready"), sem("lin_done"), sem("z_step"))
        std1_ready, out_ready = sem("std1_ready"), sem("out_ready")

        adj_rows = adj.rearrange("(t p) m -> t p m", p=P)
        x_rows = x.rearrange("(t p) d -> t p d", p=P)
        scratch_rows = scratch.rearrange("(t p) d -> t p d", p=P)
        out_rows = out.rearrange("(t p) d -> t p d", p=P)

        block = ctx.enter_context(nc.Block())

        def wait_apart(eng, semaphore, value):
            eng.wait_ge(semaphore, value)
            eng.nop(nofuse=True)

        @block.sync
        def _(sp):
            sp.dma_start(x_all, x.rearrange("(t p) d -> p t d", p=P)).then_inc(x_loaded, 16)
            for c in range(DC):
                sp.dma_start(wk[:, c], Wks[:, c * P:(c + 1) * P, :].rearrange("h p k -> p h k")
                             ).then_inc(wkv_loaded, 16)
                sp.dma_start(wv[:, c], Wvs[:, c * P:(c + 1) * P, :].rearrange("h p k -> p h k")
                             ).then_inc(wkv_loaded, 16)
                sp.dma_start(wq[:, c], Wqs[:, c * P:(c + 1) * P, :].rearrange("h p k -> p h k")
                             ).then_inc(wq_loaded, 16)
            sp.dma_start(x_tile[:, :], x_rows[0]).then_inc(xtile_loaded, 16)
            sp.wait_ge(kv_filled, H * NS + T)
            sp.dma_start(landing, adj_rows[0]).then_inc(adj_loaded, 16)
            for half in range(2):
                sp.dma_start(wreg[half * KD:(half + 1) * KD], Wo.rearrange("h k o -> k h o")
                             ).then_inc(wo_loaded, 16)

            def next_tile(t):
                sp.wait_ge(mask_ready, t * NC + NC)
                sp.dma_start(landing, adj_rows[t + 1]).then_inc(adj_loaded, 16)

            def store_tile(t):
                sp.wait_ge(y_added, t * H + H)
                sp.dma_start(scratch_rows[t], y_tile[:, :]).then_inc(y_stored, 16)

            def next_x(t):
                sp.wait_ge(y_added, t * H + 1)
                sp.dma_start(x_tile[:, :], x_rows[t + 1]).then_inc(xtile_loaded, 16)

            next_tile(0)
            next_x(0)
            with sp.Fori(1, T - 1) as t:
                next_tile(t)
                store_tile(t - 1)
                next_x(t)
            store_tile(T - 2)

            sp.wait_ge(transposed, (T * H - 1) * NS)
            for i, (w, b) in enumerate(((W_self, b_self), (W_neigh, b_neigh))):
                sp.dma_start(w_raw[i], w.rearrange("(c p) f -> p c f", p=P)).then_inc(w1_loaded, 16)
                sp.dma_start(bias_bc[i], b.rearrange("(a f) -> a f", a=1).broadcast_to([P, D])
                             ).then_inc(w1_loaded, 16)
            sp.wait_ge(scores_ready, T * H * NC)
            sp.wait_ge(y_stored, 16 * (T - 1))
            sp.dma_start(h32[:, 0:T - 1, :], scratch[0:(T - 1) * P, :].rearrange("(t p) d -> p t d", p=P)
                         ).then_inc(y_loaded, 16)
            sp.wait_ge(mask_ready, T * NC)
            sp.dma_start(mask[:, 0, :], adj_rows[0]).then_inc(adj1_loaded[0], 16)
            store_tile(T - 1)
            sp.wait_ge(y_stored, 16 * T)
            sp.dma_start(h32[:, T - 1, :], scratch_rows[T - 1]).then_inc(y_last_loaded, 16)
            sp.wait_ge(masked_ready, T * H * NC)
            sp.dma_start(mask[:, 1, :], adj_rows[1]).then_inc(adj1_loaded[1], 16)
            def next_adj(t2):
                for i in range(2):
                    sp.wait_ge(adj16_ready, 2 * t2 + i + 1)
                    sp.dma_start(mask[:, i, :], adj_rows[2 * t2 + i + 2]).then_inc(adj1_loaded[i], 16)

            def store_out(t2):
                for i in range(2):
                    sp.wait_ge(out_ready, 2 * t2 + i + 1)
                    sp.dma_start(out_rows[2 * t2 + i], o_tile[i]).then_inc(out_stored[i], 16)

            next_adj(0)
            with sp.Fori(1, T // 2 - 1) as t2:
                next_adj(t2)
                store_out(t2 - 1)
            store_out(T // 2 - 2)
            store_out(T // 2 - 1)
            for i in range(2):
                sp.wait_ge(out_stored[i], 16 * (T // 2))

        @block.gpsimd
        def _(pool):
            pool.memset(ident[:, :], 0.0).then_inc(const_step, 1)
            pool.wait_ge(const_step, 1)
            pool.affine_select(out=ident[:, :], in_=ident[:, :], compare_op=ALU.not_equal, fill=1.0,
                               base=0, pattern=[[-1, P]], channel_multiplier=1).then_inc(const_step, 1)
            pool.wait_ge(const_step, 2)
            pool.tensor_scalar(not_ident[:, :], ident[:, :], -1.0, 1.0, ALU.mult, ALU.add
                               ).then_inc(const_ready, 1)
            pool.wait_ge(const_ready, 1)

            POOL_STEPS = NC + 5

            def prepare_mask(t, c):
                cols = slice(c * CHUNK, (c + 1) * CHUNK)
                if c == 0:
                    wait_apart(pool, adj_loaded, 16 * t + 16)
                pool.tensor_scalar(landing[:, cols], landing[:, cols], -1.0, None, ALU.add
                                   ).then_inc(pool_step, 1)

            def mask_diagonal(t):
                base = POOL_STEPS * t + NC
                here = bass.ds(t * P, P)
                pool.wait_ge(pool_step, base)
                pool.tensor_copy(diag[:, :], mask[:, 0, here]).then_inc(pool_step, 1)
                wait_apart(pool, pool_step, base + 1)
                pool.tensor_scalar(diag_pos[:, :], diag[:, :], 0.0, IDENTITY_BIAS / MASK_VAL,
                                   ALU.max, ALU.add).then_inc(pool_step, 1)
                pool.wait_ge(pool_step, base + 2)
                pool.tensor_tensor(diag_pos[:, :], diag_pos[:, :], ident[:, :], ALU.mult
                                   ).then_inc(pool_step, 1)
                pool.tensor_tensor(diag[:, :], diag[:, :], not_ident[:, :], ALU.mult
                                   ).then_inc(pool_step, 1)
                wait_apart(pool, pool_step, base + 4)
                pool.tensor_tensor(mask[:, 0, here], diag[:, :], diag_pos[:, :], ALU.add
                                   ).then_inc(pool_step, 1)

            def write_mask(t, c):
                if c == 0:
                    wait_apart(pool, pool_step, POOL_STEPS * (t + 1))
                cols = slice(c * CHUNK, (c + 1) * CHUNK)
                pool.tensor_scalar(addmask[:, cols], landing[:, cols], MASK_VAL, None, ALU.mult
                                   ).then_inc(mask_ready, 1)

            def sum_parts(g):
                pool.wait_ge(parts_ready, g + 1)
                pool.tensor_tensor(head_out[:, :], head_parts[:, 0, :], head_parts[:, 1, :], ALU.add
                                   ).then_inc(head_ready, 1)

            for c in range(NC):
                prepare_mask(0, c)
            mask_diagonal(0)
            for c in range(NC):
                write_mask(0, c)

            def tile(t, first=False, last=False):
                for h in range(H):
                    if not (first and h == 0):
                        sum_parts(t * H + h - 1)
                    if h in range(1, 1 + NC) and not last:
                        prepare_mask(t + 1, h - 1)
                    if h == 5 and not last:
                        mask_diagonal(t + 1)
                    if h == 6 and not last:
                        for c in range(NC):
                            wait_apart(pool, masked_ready, (t * H + H - 1) * NC + c + 1)
                            write_mask(t + 1, c)

            tile(0, first=True)
            with pool.Fori(1, T - 1) as t:
                tile(t)
            tile(T - 1, last=True)
            sum_parts(T * H - 1)

        @block.tensor
        def _(pe):
            pe.wait_ge(const_ready, 1)
            pe.wait_ge(x_loaded, 16)
            for n in range(DC * T // BS):
                if n >= 8:
                    pe.wait_ge(xT_emptied, n - 7)
                for b in range(BS):
                    blk = n * BS + b
                    mm = pe.transpose(banks[:, n % 8, b * P:(b + 1) * P],
                                      x_all[:, blk % T, (blk // T) * P:(blk // T + 1) * P], ident[:, :])
                mm.then_inc(xT_filled, 1)

            pe.wait_ge(xT_emptied, DC * T // BS)
            pe.wait_ge(wkv_loaded, 16 * 2 * DC)
            n = 0
            for h in range(H):
                for m in range(NS):
                    if n >= 8:
                        pe.wait_ge(kv_lo, n - 7)
                    for half in range(2):
                        for c in range(DC):
                            mm = pe.matmul(banks[half * KD:(half + 1) * KD, n % 8, :], wk[:, c, h, :],
                                           xT_all[:, c, m * SUB:(m + 1) * SUB],
                                           start=(c == 0), stop=(c == DC - 1))
                    mm.then_inc(kv_filled, 1)
                    n += 1
            for t in range(T):
                pe.wait_ge(kv_lo, n - 7)
                for c in range(DC):
                    mm = pe.matmul(banks[:, n % 8, :], xT_all[:, c, t * P:(t + 1) * P],
                                   wv[:, c].rearrange("p h k -> p (h k)"),
                                   start=(c == 0), stop=(c == DC - 1))
                mm.then_inc(kv_filled, 1)
                n += 1
            pe.wait_ge(kv_lo, n)
            pe.wait_ge(wq_loaded, 16 * DC)
            pe.wait_ge(wo_loaded, 32)

            def make_xT(t):
                bank = bank_of(Q_HEADS[0], "queries")
                pe.wait_ge(xtile_loaded, 16 * t + 16)
                for c in range(DC):
                    mm = pe.transpose(bank[:, c * P:(c + 1) * P], x_tile[:, c * P:(c + 1) * P], ident[:, :])
                mm.then_inc(xT_made, 1)

            def make_q(t, part):
                bank = bank_of(Q_HEADS[1 + part], "queries")
                pe.wait_ge(xT_ready, t + 1)
                for j in range(HH):
                    for c in range(DC):
                        for half in range(2):
                            mm = pe.matmul(bank[half * KD:(half + 1) * KD, j * P:(j + 1) * P],
                                           wq[:, c, part * HH + j, :], xT_tile[:, c, :],
                                           start=(c == 0), stop=(c == DC - 1), skip_group_check=True)
                mm.then_inc(q_made, 1)

            def scores(g, h, c, t):
                if c == 0 and h % HH == 0:
                    pe.wait_ge(q_lo_ready, 2 * t + h // HH + 1)
                if not (isinstance(g, int) and g == 0 and c < 2):
                    pe.wait_ge(masked_ready, g * NC + c - 1)
                for part, q in enumerate((q_hi, q_lo)):
                    for b in range(CHUNK // SUB):
                        mm = pe.matmul(score_ps[c % 2][:, b, :], q[:, h, :],
                                       kstack[:, h, c * CHUNK + b * SUB:c * CHUNK + (b + 1) * SUB],
                                       start=(part == 0), stop=(part == 1), skip_group_check=True)
                mm.then_inc(scores_ready, 1)

            def turn(g, h, s):
                if s % 2 == 0:
                    pe.wait_ge(exp_ready, g * NC + s // 2 + 1)
                bank = bank_of(h, s)
                for b in range(BS):
                    m = s * BS + b
                    mm = pe.transpose(bank[:, b * P:(b + 1) * P], prob[:, h % 2, m * P:(m + 1) * P],
                                      ident[:, :])
                mm.then_inc(transposed, 1)

            def values(g, h, s):
                pe.wait_ge(lo_ready, g * NS + s + 1)
                for b in range(BS):
                    m = s * BS + b
                    mm = pe.matmul(av_ps, vstack[:, h, m, :],
                                   probT[:, s % NPT, b].rearrange("p s q -> p (s q)"),
                                   start=(m == 0), stop=(m == T - 1))
                mm.then_inc(av_done, 1)

            def project(g, h):
                pe.wait_ge(head_ready, g + 1)
                mm = pe.matmul(bank_of((h + 1) % H, "project")[:, 0:D], head_out[:, :], wreg[:, h, :],
                               start=True, stop=True)
                mm.then_inc(projected, 1)

            make_xT(0)
            make_q(0, 0)
            make_q(0, 1)
            for c in range(NC):
                scores(0, 0, c, 0)

            def tile(t, first=False, last=False):
                for h in range(H):
                    g = t * H + h
                    ahead = not (last and h == H - 1)
                    nh, nt = (h + 1, t) if h < H - 1 else (0, t + 1)
                    before = not (first and h == 0)
                    ph = (h - 1) % H
                    late = h in Q_HEADS
                    if ahead:
                        scores(g + 1, nh, 0, nt)
                    if before and ph in Q_HEADS and not (last and h > 0):
                        n = Q_HEADS.index(ph)
                        if n == 0:
                            pe.wait_ge(xT_ready, t + 2)
                        else:
                            pe.wait_ge(q_lo_ready, 2 * t + 2 + n if n == 1 else 2 * t + 2)
                    turn(g, h, 0)
                    if before:
                        values(g - 1, ph, 6)
                    turn(g, h, 1)
                    if before:
                        values(g - 1, ph, 7)
                    if ahead:
                        scores(g + 1, nh, 1, nt)
                    turn(g, h, 2)
                    if before:
                        pe.wait_ge(parts_ready, g)
                    values(g, h, 0)
                    turn(g, h, 3)
                    values(g, h, 1)
                    if ahead:
                        scores(g + 1, nh, 2, nt)
                    if before:
                        project(g - 1, ph)
                    pe.wait_ge(lo_ready, g * NS + 3)
                    turn(g, h, 4)
                    values(g, h, 2)
                    pe.wait_ge(lo_ready, g * NS + 4)
                    turn(g, h, 5)
                    values(g, h, 3)
                    if ahead:
                        scores(g + 1, nh, 3, nt)
                    if before:
                        pe.wait_ge(y_added, g)
                    if late and not last:
                        if h == Q_HEADS[0]:
                            make_xT(t + 1)
                        else:
                            make_q(t + 1, Q_HEADS.index(h) - 1)
                    if late:
                        pe.wait_ge(lo_ready, g * NS + 5)
                    turn(g, h, 6)
                    values(g, h, 4)
                    if late:
                        pe.wait_ge(lo_ready, g * NS + 6)
                    turn(g, h, 7)
                    values(g, h, 5)

            tile(0, first=True)
            with pe.Fori(1, T - 1) as t:
                tile(t)
            tile(T - 1, last=True)
            values(T * H - 1, H - 1, 6)
            values(T * H - 1, H - 1, 7)
            project(T * H - 1, H - 1)

            pe.wait_ge(y_added, T * H)
            pe.wait_ge(w1_loaded, 64)
            for i in range(2):
                for c in range(DC):
                    for o in range(2):
                        mm = pe.transpose(banks[:, i, c * D + o * P:c * D + (o + 1) * P],
                                          w_raw[i][:, o, c * P:(c + 1) * P], ident[:, :])
                mm.then_inc(wT_made, 1)
            pe.wait_ge(wT_ready, 2)
            for t in range(T):
                pe.wait_ge(normed, t + 1)
                if t >= 1:
                    pe.wait_ge(hT_ready, t)
                for c in range(DC):
                    mm = pe.transpose(banks[:, 2, c * P:(c + 1) * P], h32[:, t, c * P:(c + 1) * P],
                                      ident[:, :])
                mm.then_inc(hT_made, 1)
                pe.wait_ge(hT_ready, t + 1)
                if t >= 1:
                    pe.wait_ge(self_ready, t)
                for c in range(DC):
                    mm = pe.matmul(banks[:, 3, 0:D], hT[:, c, :], wT[0][:, c, :],
                                   start=(c == 0), stop=(c == DC - 1))
                mm.then_inc(self_made, 1)

            def turn_adj(t, i, k):
                if k == 0:
                    pe.wait_ge(adj16_ready, t + 1)
                if not (isinstance(t, int) and t == 0):
                    pe.wait_ge(adjT_by_act if k % 2 == 0 else adjT_by_dve, 2 * t + k // 2 - 1)
                bank = banks[:, k, :].bitcast(F16)
                for b in range(8):
                    m = 8 * k + b
                    mm = pe.transpose(bank[:, b * P:(b + 1) * P], adj16[i][:, m * P:(m + 1) * P],
                                      ident16[:, :])
                mm.then_inc(adjT_made, 1)

            def aggregate(t, i, k):
                pe.wait_ge(adjT_by_act if k % 2 == 0 else adjT_by_dve, 2 * t + k // 2 + 1)
                for b in range(8):
                    m = 8 * k + b
                    mm = pe.matmul(banks[:, 4 + i, :], adjT[i][:, m * P:(m + 1) * P],
                                   hsplit[:, m].rearrange("p s d -> p (s d)"),
                                   start=(m == 0), stop=(m == T - 1))
                if k == 3:
                    mm.then_inc(agg_done, 1)

            def turn_neigh(t, i):
                pe.wait_ge(h_neigh_ready, t + 1)
                for c in range(DC):
                    mm = pe.transpose(banks[:, 6, c * P:(c + 1) * P], h_neigh[i][:, c * P:(c + 1) * P],
                                      ident[:, :])
                mm.then_inc(hnT_made, 1)

            def linear(t, i):
                pe.wait_ge(hnT_ready, t + 1)
                for c in range(DC):
                    mm = pe.matmul(banks[:, 7, 0:D], hnT[i][:, c, :], wT[1][:, c, :],
                                   start=(c == 0), stop=(c == DC - 1))
                mm.then_inc(lin_done, 1)

            pe.wait_ge(self_ready, T)
            pe.wait_ge(h_lo_ready, T)
            pe.wait_ge(ident16_ready, 1)
            for k in range(4):
                turn_adj(0, 0, k)

            def pair(t2, first=False, last=False):
                for i in range(2):
                    t = 2 * t2 + i
                    more = not (last and i == 1)
                    before = not (first and i == 0)
                    for k in range(4):
                        if more:
                            turn_adj(t + 1, 1 - i, k)
                        if k == 0 and t2 != 0 if isinstance(t2, int) else k == 0:
                            pe.wait_ge(h_neigh_ready, t - 1)
                        aggregate(t, i, k)
                        if k == 0 and before:
                            turn_neigh(t - 1, 1 - i)
                        if k == 2 and before:
                            linear(t - 1, 1 - i)

            pair(0, first=True)
            with pe.Fori(1, T // 2 - 1) as t2:
                pair(t2)
            pair(T // 2 - 1, last=True)
            turn_neigh(T - 1, 1)
            linear(T - 1, 1)

        @block.scalar
        def _(act):
            for n in range(DC * T // BS):
                act.wait_ge(xT_filled, n + 1)
                blk = n * BS
                act.activation(xT_all[:, blk // T, (blk % T) * P:(blk % T + BS) * P], banks[:, n % 8, :],
                               ACT.Copy).then_inc(xT_emptied, 1)
            n = 0
            for h in range(H):
                for m in range(NS):
                    act.wait_ge(kv_filled, n + 1)
                    act.activation(kstack[:, h, m * SUB:(m + 1) * SUB], banks[:, n % 8, :], ACT.Copy
                                   ).then_inc(kv_hi, 1)
                    n += 1
            for t in range(T):
                act.wait_ge(kv_filled, n + 1)
                act.activation(vstack[:, :, t, 0:KD], banks[:, n % 8, :].rearrange("p (h k) -> p h k", h=H),
                               ACT.Copy).then_inc(kv_hi, 1)
                n += 1

            def copy_xT(t):
                act.wait_ge(xT_made, t + 1)
                act.activation(xT_tile[:, :, :].rearrange("p c q -> p (c q)"),
                               bank_of(Q_HEADS[0], "queries")[:, 0:D], ACT.Copy).then_inc(xT_ready, 1)

            def high_q(t, part):
                act.wait_ge(q_made, 2 * t + part + 1)
                act.activation(q_hi[:, part * HH:(part + 1) * HH, :].rearrange("p h q -> p (h q)"),
                               bank_of(Q_HEADS[1 + part], "queries"), ACT.Copy, scale=SCALE
                               ).then_inc(q_hi_ready, 1)

            def exps(g, h, c):
                if c == 0:
                    act.wait_ge(neg_max_ready, g + 1)
                cols = prob[:, h % 2, c * CHUNK:(c + 1) * CHUNK]
                act.activation(cols, cols, ACT.Exp, bias=neg_max[:, h % 2:h % 2 + 1],
                               accum_out=chunk_sum[:, h % 2, c:c + 1]).then_inc(exp_ready, 1)

            def high(g, h, s):
                act.wait_ge(transposed, g * NS + s + 1)
                act.activation(probT[:, s % NPT, :, 0, :], bank_of(h, s).rearrange("p (b q) -> p b q", b=BS),
                               ACT.Copy).then_inc(hi_ready, 1)

            def take_parts(g):
                act.wait_ge(av_done, g * NS + NS)
                act.activation(head_parts[:, :, :].rearrange("p s q -> p (s q)"), av_ps, ACT.Copy
                               ).then_inc(parts_ready, 1)

            copy_xT(0)
            high_q(0, 0)
            high_q(0, 1)
            exps(0, 0, 0)

            def tile(t, first=False, last=False):
                for h in range(H):
                    g = t * H + h
                    exps(g, h, 1)
                    high(g, h, 0)
                    high(g, h, 1)
                    if not (first and h == 0):
                        take_parts(g - 1)
                    exps(g, h, 2)
                    high(g, h, 2)
                    high(g, h, 3)
                    exps(g, h, 3)
                    high(g, h, 4)
                    high(g, h, 5)
                    if h in Q_HEADS and not last:
                        if h == Q_HEADS[0]:
                            copy_xT(t + 1)
                        else:
                            high_q(t + 1, Q_HEADS.index(h) - 1)
                    high(g, h, 6)
                    high(g, h, 7)
                    if not (last and h == H - 1):
                        exps(g + 1, h + 1, 0)

            tile(0, first=True)
            with act.Fori(1, T - 1) as t:
                tile(t)
            tile(T - 1, last=True)
            take_parts(T * H - 1)

            for i in range(2):
                act.wait_ge(wT_made, i + 1)
                act.activation(wT[i].rearrange("p c o -> p (c o)"), banks[:, i, :], ACT.Copy
                               ).then_inc(wT_ready, 1)
            act.wait_ge(eps_ready, 1)
            act.wait_ge(mv_ready, T)
            act.activation(std_all, mean_var[:, :, 1], ACT.Sqrt, bias=eps_col).then_inc(std_ready, 1)
            for t in range(T):
                act.wait_ge(normed, t + 1)
                act.activation(hsplit[:, t, 0, :], h32[:, t, :], ACT.Copy).then_inc(h_hi_ready, 1)
                act.wait_ge(hT_made, t + 1)
                if t >= 1:
                    act.wait_ge(self_made, t)
                act.activation(hT.rearrange("p c q -> p (c q)"), banks[:, 2, 0:D], ACT.Copy
                               ).then_inc(hT_ready, 1)

            def convert(t, i, t2):
                act.wait_ge(adj1_loaded[i], 16 * t2 + 16)
                if not (isinstance(t, int) and t < 2):
                    act.wait_ge(adjT_made, 4 * t - 4)
                    act.wait_ge(inv_deg_ready, 2 * t - 2)
                act.activation(adj16[i], mask[:, i, :], ACT.Copy, accum_out=deg_raw[i]
                               ).then_inc(adj16_ready, 1)

            def empty_adj(t, i, k):
                act.wait_ge(adjT_made, 4 * t + k + 1)
                if not (isinstance(t, int) and t < 2):
                    act.wait_ge(agg_done, t - 1)
                act.activation(adjT[i][:, 8 * k * P:8 * (k + 1) * P], banks[:, k, :].bitcast(F16), ACT.Copy
                               ).then_inc(adjT_by_act, 1)

            def scale_low(t, i):
                act.wait_ge(agg_done, t + 1)
                act.wait_ge(inv_deg_ready, 2 * t + 2)
                act.activation(agg_lo[i], banks[:, 4 + i, D:2 * D], ACT.Copy, scale=inv_deg[i]
                               ).then_inc(agg_lo_ready, 1)

            def copy_neigh(t, i):
                act.wait_ge(hnT_made, t + 1)
                act.activation(hnT[i].rearrange("p c q -> p (c q)"), banks[:, 6, 0:D], ACT.Copy
                               ).then_inc(hnT_ready, 1)

            def deviation(t, i):
                act.wait_ge(z_step, 4 * t + 4)
                act.activation(std1[i], mean_var1[i][:, 1:2], ACT.Sqrt, bias=eps_col).then_inc(std1_ready, 1)

            convert(0, 0, 0)
            empty_adj(0, 0, 0)
            empty_adj(0, 0, 2)
            convert(1, 1, 0)

            def pair(t2, first=False, last=False):
                for i in range(2):
                    t = 2 * t2 + i
                    more = not (last and i == 1)
                    before = not (first and i == 0)
                    if before:
                        scale_low(t - 1, 1 - i)
                    if more:
                        empty_adj(t + 1, 1 - i, 0)
                    if before:
                        copy_neigh(t - 1, 1 - i)
                    if more:
                        empty_adj(t + 1, 1 - i, 2)
                    if not last:
                        convert(t + 2, i, t2 + 1)
                    if before:
                        deviation(t - 1, 1 - i)

            pair(0, first=True)
            with act.Fori(1, T // 2 - 1) as t2:
                pair(t2)
            pair(T // 2 - 1, last=True)
            scale_low(T - 1, 1)
            copy_neigh(T - 1, 1)
            deviation(T - 1, 1)

        @block.vector
        def _(dve):
            n = 0
            for h in range(H):
                for m in range(NS):
                    dve.wait_ge(kv_hi, n + 1)
                    low = kstack[KD:P, h, m * SUB:(m + 1) * SUB]
                    dve.tensor_tensor(low, banks[KD:P, n % 8, :], low, ALU.subtract).then_inc(kv_lo, 1)
                    n += 1
            for t in range(T):
                dve.wait_ge(kv_hi, n + 1)
                dve.tensor_tensor(vstack[:, :, t, KD:P], banks[:, n % 8, :].rearrange("p (h k) -> p h k", h=H),
                                  vstack[:, :, t, 0:KD], ALU.subtract).then_inc(kv_lo, 1)
                n += 1

            def low_q(t, part):
                dve.wait_ge(q_hi_ready, 2 * t + part + 1)
                heads = slice(part * HH, (part + 1) * HH)
                dve.scalar_tensor_tensor(out=q_lo[:, heads, :].rearrange("p h q -> p (h q)"),
                                         in0=bank_of(Q_HEADS[1 + part], "queries"), scalar=SCALE,
                                         in1=q_hi[:, heads, :].rearrange("p h q -> p (h q)"),
                                         op0=ALU.mult, op1=ALU.subtract).then_inc(q_lo_ready, 1)

            def add_mask(g, h, c, t):
                if h == 0:
                    wait_apart(dve, mask_ready, t * NC + c + 1)
                wait_apart(dve, scores_ready, g * NC + c + 1)
                cols = slice(c * CHUNK, (c + 1) * CHUNK)
                dve.tensor_tensor_reduce(prob[:, h % 2, cols],
                                         score_ps[c % 2].rearrange("p b n -> p (b n)"), addmask[:, cols],
                                         1.0, LOWEST, ALU.add, ALU.max,
                                         chunk_max[:, h % 2, c:c + 1]).then_inc(masked_ready, 1)

            def max_of_row(g, h):
                dve.wait_ge(masked_ready, g * NC + NC)
                dve.tensor_reduce(neg_max[:, h % 2:h % 2 + 1], chunk_max[:, h % 2, :], AX.X, ALU.max,
                                  negate=True).then_inc(neg_max_ready, 1)

            def low(g, h, s):
                dve.wait_ge(hi_ready, g * NS + s + 1)
                dve.tensor_tensor(probT[:, s % NPT, :, 1, :], bank_of(h, s).rearrange("p (b q) -> p b q", b=BS),
                                  probT[:, s % NPT, :, 0, :], ALU.subtract).then_inc(lo_ready, 1)

            def sum_row(g, h):
                dve.wait_ge(exp_ready, g * NC + NC)
                dve.tensor_reduce(row_sum[:, :], chunk_sum[:, h % 2, :], AX.X, ALU.add).then_inc(sum_ready, 1)

            def invert_sum(g):
                dve.wait_ge(sum_ready, g + 1)
                dve.reciprocal(inv_sum[:, :], row_sum[:, :]).then_inc(inv_ready, 1)

            def add_head(g, h, t):
                dve.wait_ge(projected, g + 1)
                dve.wait_ge(inv_ready, g + 1)
                if h > 0:
                    dve.wait_ge(y_added, g)
                else:
                    dve.wait_ge(xtile_loaded, 16 * t + 16)
                    if not (isinstance(t, int) and t == 0):
                        dve.wait_ge(y_stored, 16 * t)
                dve.scalar_tensor_tensor(out=y_tile[:, :], in0=bank_of((h + 1) % H, "project")[:, 0:D],
                                         scalar=inv_sum[:, 0:1],
                                         in1=x_tile[:, :] if h == 0 else y_tile[:, :],
                                         op0=ALU.mult, op1=ALU.add).then_inc(y_added, 1)

            low_q(0, 0)
            low_q(0, 1)
            for c in range(NC):
                add_mask(0, 0, c, 0)
            max_of_row(0, 0)

            def tile(t, first=False, last=False):
                for h in range(H):
                    g = t * H + h
                    ahead = not (last and h == H - 1)
                    nh, nt = (h + 1, t) if h < H - 1 else (0, t + 1)
                    if ahead:
                        add_mask(g + 1, nh, 0, nt)
                    low(g, h, 0)
                    low(g, h, 1)
                    if ahead:
                        add_mask(g + 1, nh, 1, nt)
                    low(g, h, 2)
                    low(g, h, 3)
                    if ahead:
                        add_mask(g + 1, nh, 2, nt)
                    if not (first and h == 0):
                        add_head(g - 1, (h - 1) % H, t)
                    sum_row(g, h)
                    low(g, h, 4)
                    invert_sum(g)
                    low(g, h, 5)
                    if ahead:
                        add_mask(g + 1, nh, 3, nt)
                        max_of_row(g + 1, nh)
                    if h in Q_HEADS[1:] and not last:
                        low_q(t + 1, Q_HEADS.index(h) - 1)
                    low(g, h, 6)
                    low(g, h, 7)

            tile(0, first=True)
            with dve.Fori(1, T - 1) as t:
                tile(t)
            tile(T - 1, last=True)
            add_head(T * H - 1, H - 1, T - 1)

            dve.memset(eps_col, LN_EPS).then_inc(eps_ready, 1)
            dve.tensor_copy(ident16, ident[:, :]).then_inc(ident16_ready, 1)
            dve.wait_ge(y_loaded, 16)
            for t in range(T + 1):
                if t < T:
                    if t == T - 1:
                        dve.wait_ge(y_last_loaded, 16)
                    dve.bn_stats(stats[:, t, :], h32[:, t, :]).then_inc(stats_ready, 1)
                if t > 0:
                    dve.wait_ge(stats_ready, t)
                    dve.bn_aggr(mean_var[:, t - 1, :], stats[:, t - 1, :]).then_inc(mv_ready, 1)
            dve.wait_ge(w1_loaded, 64)
            dve.tensor_tensor(bias_sum, bias_bc[0], bias_bc[1], ALU.add).then_inc(bias_ready, 1)
            dve.wait_ge(std_ready, 1)
            dve.reciprocal(inv_std_all, std_all).then_inc(inv_std_ready, 1)
            dve.wait_ge(inv_std_ready, 1)
            dve.wait_ge(mv_ready, T)
            dve.wait_ge(bias_ready, 1)
            AHEAD = 2
            for t in range(T + AHEAD):
                if t < T:
                    dve.tensor_scalar(h32[:, t, :], h32[:, t, :], mean_var[:, t, 0:1],
                                      inv_std_all[:, t:t + 1], ALU.subtract, ALU.mult).then_inc(normed, 1)
                if t >= AHEAD:
                    u = t - AHEAD
                    dve.wait_ge(h_hi_ready, u + 1)
                    dve.tensor_tensor(hsplit[:, u, 1, :], h32[:, u, :], hsplit[:, u, 0, :], ALU.subtract
                                      ).then_inc(h_lo_ready, 1)
                    dve.wait_ge(self_made, u + 1)
                    dve.tensor_tensor(self_term[:, u, :], banks[:, 3, 0:D], bias_sum, ALU.add
                                      ).then_inc(self_ready, 1)

            def degree(t, i):
                dve.wait_ge(adj16_ready, t + 1)
                if not (isinstance(t, int) and t < 2):
                    dve.wait_ge(h_neigh_ready, t - 1)
                dve.tensor_scalar(deg[i], deg_raw[i], DEG_EPS, None, ALU.add).then_inc(inv_deg_ready, 1)
                dve.wait_ge(inv_deg_ready, 2 * t + 1)
                dve.reciprocal(inv_deg[i], deg[i]).then_inc(inv_deg_ready, 1)

            def empty_adj(t, i, k):
                dve.wait_ge(adjT_made, 4 * t + k + 1)
                if not (isinstance(t, int) and t < 2):
                    dve.wait_ge(agg_done, t - 1)
                dve.tensor_copy(adjT[i][:, 8 * k * P:8 * (k + 1) * P], banks[:, k, :].bitcast(F16)
                                ).then_inc(adjT_by_dve, 1)

            def neighbours(t, i):
                dve.wait_ge(agg_lo_ready, t + 1)
                dve.scalar_tensor_tensor(out=h_neigh[i], in0=banks[:, 4 + i, 0:D], scalar=inv_deg[i],
                                         in1=agg_lo[i], op0=ALU.mult, op1=ALU.add).then_inc(h_neigh_ready, 1)

            def add_and_relu(t, i):
                dve.wait_ge(lin_done, t + 1)
                dve.tensor_tensor(z[i], banks[:, 7, 0:D], self_term[:, t, :], ALU.add).then_inc(z_step, 1)
                dve.wait_ge(z_step, 4 * t + 1)
                dve.scalar_tensor_tensor(out=z[i], in0=z[i], scalar=0.0, in1=h32[:, t, :],
                                         op0=ALU.max, op1=ALU.add).then_inc(z_step, 1)
                dve.wait_ge(z_step, 4 * t + 2)
                dve.bn_stats(stats1[i], z[i]).then_inc(z_step, 1)
                wait_apart(dve, z_step, 4 * t + 3)
                dve.bn_aggr(mean_var1[i], stats1[i]).then_inc(z_step, 1)

            def normalise(t, i, stored):
                dve.wait_ge(std1_ready, t + 1)
                dve.reciprocal(inv_std1[i], std1[i]).then_inc(inv_std_ready, 1)
                dve.wait_ge(inv_std_ready, t + 2)
                if not (isinstance(stored, int) and stored <= 0):
                    dve.wait_ge(out_stored[i], 16 * stored)
                dve.tensor_scalar(o_tile[i], z[i], mean_var1[i][:, 0:1], inv_std1[i],
                                  ALU.subtract, ALU.mult).then_inc(out_ready, 1)

            degree(0, 0)
            empty_adj(0, 0, 1)
            empty_adj(0, 0, 3)

            def pair(t2, first=False, last=False):
                for i in range(2):
                    t = 2 * t2 + i
                    more = not (last and i == 1)
                    if not (first and i == 0):
                        neighbours(t - 1, 1 - i)
                    if more:
                        degree(t + 1, 1 - i)
                        empty_adj(t + 1, 1 - i, 1)
                        empty_adj(t + 1, 1 - i, 3)
                    if not (first and i == 0):
                        add_and_relu(t - 1, 1 - i)
                        normalise(t - 1, 1 - i, t2 - 1 + i)

            pair(0, first=True)
            with dve.Fori(1, T // 2 - 1) as t2:
                pair(t2)
            pair(T // 2 - 1, last=True)
            neighbours(T - 1, 1)
            add_and_relu(T - 1, 1)
            normalise(T - 1, 1, T // 2 - 1)


_INS = ['x', 'adj', 'L0_gnn_Wks', 'L0_gnn_Wqs', 'L0_gnn_Wvs', 'L0_gnn_Wo',
        'L1_gnn_W_neigh', 'L1_gnn_b_neigh', 'L1_gnn_W_self', 'L1_gnn_b_self']
_OUTS = [((4096, 256), 'float32')]


def kernel(**inputs):
    import numpy as _np
    import concourse.bacc as _bacc
    from concourse import mybir as _mybir
    from concourse.bass_utils import run_bass_kernel_spmd as _run

    nc = _bacc.Bacc("TRN2", target_bir_lowering=False, num_devices=1, dynamic_dma_scratch_size=1024)
    arrays, args = {}, []
    for name in _INS:
        a = _np.ascontiguousarray(inputs[name])
        arrays[f"in_{name}_dram"] = a
        args.append(nc.dram_tensor(f"in_{name}_dram", a.shape, _mybir.dt.from_np(a.dtype), kind="ExternalInput").ap())
    for i, (shape, dtype) in enumerate(_OUTS):
        dt = _mybir.dt.from_np(_np.dtype(dtype))
        args.append(nc.dram_tensor(f"out_{i}_dram", shape, dt, kind="ExternalOutput").ap())
    gnn_two_layers(nc, *args)
    r = _run(nc, [arrays], core_ids=[0])
    got = tuple(r.results[0][f"out_{i}_dram"] for i in range(len(_OUTS)))
    return got[0]
```

```python
from contextlib import ExitStack

import concourse.bass as bass
from concourse import mybir

P = 128
CHUNK = 1024
SUB = 512
LN_EPS = 1e-5
DEG_EPS = 1e-5
MASK_VAL = 1e16
IDENTITY_BIAS = 0.01
LOWEST = -3.0e38

ALU = mybir.AluOpType
ACT = mybir.ActivationFunctionType
AX = mybir.AxisListType
F32 = mybir.dt.float32
F16 = mybir.dt.float16


def gnn_two_layers(nc, x, adj, Wks, Wqs, Wvs, Wo, W_neigh, b_neigh, W_self, b_self, out):
    N, D = x.shape
    H, _, KD = Wks.shape
    T = N // P
    DC = D // P
    NC = N // CHUNK
    NS = N // SUB
    BS = SUB // P
    SCALE = float(KD) ** -0.5
    HH = H // 2
    NPT = 4
    Q_HEADS = (3, 4, 7)
    assert 2 * KD == P and D == 2 * P and NC == 4 and NS == 8 and H == 8

    scratch = nc.dram_tensor("x_plus_attention", [N, D], F32, kind="Internal").ap()

    with ExitStack() as ctx:
        def sb(name, shape, dt):
            return ctx.enter_context(nc.sbuf_tensor(name, shape, dt))

        def sem(name):
            return ctx.enter_context(nc.semaphore(name))

        kstack = sb("kstack", [P, H, N], F16)
        vstack = sb("vstack", [P, H, T, P], F16)
        prob = sb("prob", [P, 2, N], F32)
        mask = sb("mask", [P, 2, N], F32)
        probT = sb("probT", [P, NPT, BS, 2, P], F16)
        q_hi = sb("q_hi", [P, H, P], F16)
        q_lo = sb("q_lo", [P, H, P], F16)
        wq = sb("wq", [P, DC, H, KD], F32)
        wreg = sb("wreg", [P, H, D], F32)
        x_tile = sb("x_tile", [P, D], F32)
        xT_tile = sb("xT_tile", [P, DC, P], F32)
        y_tile = sb("y_tile", [P, D], F32)
        head_parts = sb("head_parts", [P, 2, P], F32)
        head_out = sb("head_out", [P, P], F32)
        diag = sb("diag", [P, P], F32)
        diag_pos = sb("diag_pos", [P, P], F32)
        ident = sb("ident", [P, P], F32)
        y_stat = sb("y_stat", [P, 6], F32)
        y_mean_var = sb("y_mean_var", [P, 2], F32)
        mean_var = sb("mean_var", [P, T, 2], F32)
        chunk_max = sb("chunk_max", [P, 2, NC], F32)
        neg_max = sb("neg_max", [P, 2], F32)
        chunk_sum = sb("chunk_sum", [P, 2, NC], F32)
        row_sum = sb("row_sum", [P, 1], F32)
        inv_sum = sb("inv_sum", [P, 1], F32)
        landing, addmask = mask[:, 0, :], mask[:, 1, :]
        vflat = vstack[:, :, :, :].rearrange("p h t k -> p (h t k)")
        x_all = vflat[:, 0:2 * T * D].bitcast(F32).rearrange("p (t d) -> p t d", d=D)
        k_pair = vflat[:, 2 * T * D:2 * T * D + 4 * N].rearrange(
            "p (i s n) -> p i s n", i=2, s=2)
        xT_all = prob
        wflat = wreg[:, :, :].rearrange("p h d -> p (h d)")
        wk = wflat[:, 0:DC * H * KD].rearrange("p (c h k) -> p c h k", c=DC, h=H)
        wv = wflat[:, DC * H * KD:2 * DC * H * KD].rearrange("p (c h k) -> p c h k", c=DC, h=H)

        kflat = kstack[:, :, :].rearrange("p h n -> p (h n)")
        h32 = kflat[:, 0:2 * T * D].bitcast(F32).rearrange("p (t d) -> p t d", d=D)
        self_term = kflat[:, 2 * T * D:4 * T * D].bitcast(F32).rearrange("p (t d) -> p t d", d=D)
        gsplit = vflat[:, 0:2 * T * D].rearrange("p (t s d) -> p t s d", t=T, s=2)
        adj16 = [vflat[:, 2 * T * D + i * N:2 * T * D + (i + 1) * N] for i in range(2)]
        adjT = [vflat[:, 2 * T * D + (2 + i) * N:2 * T * D + (3 + i) * N] for i in range(2)]
        pflat = prob[:, :, :].rearrange("p a n -> p (a n)")

        def carve(first, *shape):
            n = 1
            for s in shape:
                n *= s
            v = pflat[:, first:first + n]
            return v if len(shape) == 1 else v.rearrange("p (a b) -> p a b", a=shape[0])

        w_raw = [carve(0, 2, D), carve(512, 2, D)]
        wT = carve(1024, DC, 2 * D)
        bias_bc = [carve(2048, D), carve(2304, D)]
        bias_sum = carve(2560, D)
        hT = [carve(2816 + i * D, DC, P) for i in range(2)]
        std_all = carve(3328, T)
        inv_std_all = carve(3360, T)
        agg_lo = [carve(3392 + i * D, D) for i in range(2)]
        neigh = [carve(3904 + i * D, D) for i in range(2)]
        z = [carve(4928 + i * D, D) for i in range(2)]
        o_tile = [carve(5440 + i * D, D) for i in range(2)]
        deg = [carve(5952 + i, 1) for i in range(2)]
        inv_deg = [carve(5956 + i, 1) for i in range(2)]
        stats1 = [carve(5960 + 8 * i, 6) for i in range(2)]
        mean_var1 = [carve(5976 + 2 * i, 2) for i in range(2)]
        std1 = [carve(5980 + i, 1) for i in range(2)]
        inv_std1 = [carve(5984 + i, 1) for i in range(2)]
        eps_col = carve(5988, 1)
        deg_raw = [carve(5990 + i, 1) for i in range(2)]
        deg_part = [carve(5992 + NC * i, NC) for i in range(2)]
        ident16 = carve(6016, P // 2).bitcast(F16)

        banks = ctx.enter_context(nc.psum_tensor("banks", [P, 8, 512], F32))
        score_ps = [banks[:, 2 * i:2 * i + 2, :] for i in range(2)]
        turn_ps = [banks[:, 4 + i, :] for i in range(3)]
        av_ps = banks[:, 7, 0:2 * P]

        def bank_of(h, use):
            before = sum(q < h for q in Q_HEADS)
            late = int(h in Q_HEADS)
            place = {"project": 4, "queries": 5}.get(use)
            if place is None:
                place = use if use < 4 else use + 1 + late
            return turn_ps[((NS + 1) * h + before + place) % 3]
        assert (H * (NS + 1) + len(Q_HEADS)) % 3 == 0

        x_loaded = [sem(f"x_loaded_{i}") for i in range(4)]
        wkv_loaded, wq_loaded, wo_loaded = sem("wkv_loaded"), sem("wq_loaded"), sem("wo_loaded")
        xtile_loaded, adj_loaded, y_stored = sem("xtile_loaded"), sem("adj_loaded"), sem("y_stored")
        const_ready, const_step = sem("const_ready"), sem("const_step")
        xT_filled, xT_emptied = sem("xT_filled"), sem("xT_emptied")
        kv_filled, kv_hi, kv_lo = sem("kv_filled"), sem("kv_hi"), sem("kv_lo")
        k_spread = [sem(f"k_spread_{i}") for i in range(2)]
        q_spread = [sem(f"q_spread_{i}") for i in range(2)]
        scores_ready, masked_ready, neg_max_ready = (
            sem("scores_ready"), sem("masked_ready"), sem("neg_max_ready"))
        exp_ready, transposed = sem("exp_ready"), sem("transposed")
        hi_ready, lo_ready, av_done = sem("hi_ready"), sem("lo_ready"), sem("av_done")
        parts_ready, head_ready, projected, y_added = (
            sem("parts_ready"), sem("head_ready"), sem("projected"), sem("y_added"))
        sum_ready, inv_ready = sem("sum_ready"), sem("inv_ready")
        xT_made, xT_ready = sem("xT_made"), sem("xT_ready")
        q_made, q_hi_ready, q_lo_ready = sem("q_made"), sem("q_hi_ready"), sem("q_lo_ready")
        pool_step, mask_ready = sem("pool_step"), sem("mask_ready")
        y_loaded = [sem(f"y_loaded_{i}") for i in range(4)]
        y_last_loaded, w1_loaded = sem("y_last_loaded"), sem("w1_loaded")
        adj1_loaded = [sem(f"adj1_loaded_{i}") for i in range(2)]
        out_stored = [sem(f"out_stored_{i}") for i in range(2)]
        mv_kept = sem("mv_kept")
        stats_ready, mv_ready, std_ready, inv_std_ready, normed = (
            sem("stats_ready"), sem("mv_ready"), sem("std_ready"), sem("inv_std_ready"), sem("normed"))
        eps_ready, bias_ready, ident16_ready = sem("eps_ready"), sem("bias_ready"), sem("ident16_ready")
        g_hi_ready, g_lo_ready = sem("g_hi_ready"), sem("g_lo_ready")
        wT_made, wT_ready = sem("wT_made"), sem("wT_ready")
        hT_made, hT_ready, linear_made, self_ready = (
            sem("hT_made"), sem("hT_ready"), sem("linear_made"), sem("self_ready"))
        adj16_ready, adjT_made, adjT_by_act, adjT_by_dve = (
            sem("adj16_ready"), sem("adjT_made"), sem("adjT_by_act"), sem("adjT_by_dve"))
        agg_done, agg_lo_ready, deg_part_ready, deg_raw_ready, inv_deg_ready, neigh_ready, z_step = (
            sem("agg_done"), sem("agg_lo_ready"), sem("deg_part_ready"), sem("deg_raw_ready"),
            sem("inv_deg_ready"), sem("neigh_ready"), sem("z_step"))
        std1_ready, out_ready = sem("std1_ready"), sem("out_ready")

        adj_rows = adj.rearrange("(t p) m -> t p m", p=P)
        x_rows = x.rearrange("(t p) d -> t p d", p=P)
        scratch_rows = scratch.rearrange("(t p) d -> t p d", p=P)
        out_rows = out.rearrange("(t p) d -> t p d", p=P)

        block = ctx.enter_context(nc.Block())

        def wait_apart(eng, semaphore, value):
            eng.wait_ge(semaphore, value)
            eng.nop(nofuse=True)

        @block.sync
        def _(sp):
            for i in range(4):
                sp.dma_start(x_all[:, i * T // 4:(i + 1) * T // 4, :],
                             x[i * N // 4:(i + 1) * N // 4, :].rearrange("(t p) d -> p t d", p=P)
                             ).then_inc(x_loaded[i], 16)
            for c in range(DC):
                sp.dma_start(wk[:, c], Wks[:, c * P:(c + 1) * P, :].rearrange("h p k -> p h k")
                             ).then_inc(wkv_loaded, 16)
                sp.dma_start(wv[:, c], Wvs[:, c * P:(c + 1) * P, :].rearrange("h p k -> p h k")
                             ).then_inc(wkv_loaded, 16)
                sp.dma_start(wq[:, c], Wqs[:, c * P:(c + 1) * P, :].rearrange("h p k -> p h k")
                             ).then_inc(wq_loaded, 16)
            sp.dma_start(x_tile[:, :], x_rows[0]).then_inc(xtile_loaded, 16)
            sp.dma_start(landing, adj_rows[0]).then_inc(adj_loaded, 16)
            def spread_q(t, part):
                sp.wait_ge(q_lo_ready, 2 * t + part + 1)
                even = slice(part * HH, (part + 1) * HH, 2)
                odd = slice(part * HH + 1, (part + 1) * HH, 2)
                for q in (q_hi, q_lo):
                    for half in range(2):
                        sp.dma_start(q[half * KD:(half + 1) * KD, odd, :], q[KD:P, even, :]
                                     ).then_inc(q_spread[part], 16)
                sp.wait_ge(q_spread[part], 96 * t + 64)
                for q in (q_hi, q_lo):
                    sp.dma_start(q[KD:P, even, :], q[0:KD, even, :]).then_inc(q_spread[part], 16)

            for part in range(2):
                spread_q(0, part)
            for j in range(H // 2):
                for s, ready in enumerate((kv_hi, kv_lo)):
                    sp.wait_ge(ready, (j + 1) * NS)
                    for e in range(2):
                        sp.dma_start(kstack[s * KD:(s + 1) * KD, 2 * j + e, :],
                                     k_pair[e * KD:(e + 1) * KD, j % 2, s, :]).then_inc(k_spread[j % 2], 16)
            sp.wait_ge(kv_filled, H // 2 * NS + T)
            for half in range(2):
                sp.dma_start(wreg[half * KD:(half + 1) * KD], Wo.rearrange("h k o -> k h o")
                             ).then_inc(wo_loaded, 16)

            def next_tile(t):
                sp.wait_ge(mask_ready, t * NC + NC)
                sp.dma_start(landing, adj_rows[t + 1]).then_inc(adj_loaded, 16)

            def store_tile(t):
                sp.wait_ge(y_added, t * H + H)
                sp.dma_start(scratch_rows[t], y_tile[:, :]).then_inc(y_stored, 16)

            def next_x(t):
                sp.wait_ge(y_added, t * H + 1)
                sp.dma_start(x_tile[:, :], x_rows[t + 1]).then_inc(xtile_loaded, 16)

            def next_q(t):
                for part in range(2):
                    spread_q(t + 1, part)

            next_tile(0)
            next_x(0)
            next_q(0)
            with sp.Fori(1, T - 1) as t:
                next_tile(t)
                store_tile(t - 1)
                next_x(t)
                next_q(t)
            store_tile(T - 2)

            sp.wait_ge(transposed, (T * H - 1) * NS)
            for i, (w, b) in enumerate(((W_self, b_self), (W_neigh, b_neigh))):
                sp.dma_start(w_raw[i], w.rearrange("(c p) f -> p c f", p=P)).then_inc(w1_loaded, 16)
                sp.dma_start(bias_bc[i], b.rearrange("(a f) -> a f", a=1).broadcast_to([P, D])
                             ).then_inc(w1_loaded, 16)
            sp.wait_ge(scores_ready, T * H * NC)
            sp.wait_ge(y_stored, 16 * (T - 1))
            for i in range(4):
                a, b = i * T // 4, min((i + 1) * T // 4, T - 1)
                sp.dma_start(h32[:, a:b, :], scratch[a * P:b * P, :].rearrange("(t p) d -> p t d", p=P)
                             ).then_inc(y_loaded[i], 16)
            sp.wait_ge(mask_ready, T * NC)
            sp.dma_start(mask[:, 0, :], adj_rows[0]).then_inc(adj1_loaded[0], 16)
            store_tile(T - 1)
            sp.wait_ge(y_stored, 16 * T)
            sp.dma_start(h32[:, T - 1, :], scratch_rows[T - 1]).then_inc(y_last_loaded, 16)
            sp.wait_ge(masked_ready, T * H * NC)
            sp.dma_start(mask[:, 1, :], adj_rows[1]).then_inc(adj1_loaded[1], 16)
            def next_adj(t2):
                for i in range(2):
                    if isinstance(t2, int) and t2 == 0:
                        sp.wait_ge(deg_part_ready, NC * (i + 1))
                    else:
                        sp.wait_ge(adj16_ready, 2 * t2 + i - 1)
                    sp.dma_start(mask[:, i, :], adj_rows[2 * t2 + i + 2]).then_inc(adj1_loaded[i], 16)

            def store_out(t2):
                for i in range(2):
                    sp.wait_ge(out_ready, 2 * t2 + i + 1)
                    sp.dma_start(out_rows[2 * t2 + i], o_tile[i]).then_inc(out_stored[i], 16)

            next_adj(0)
            with sp.Fori(1, T // 2 - 1) as t2:
                next_adj(t2)
                store_out(t2 - 1)
            store_out(T // 2 - 2)
            store_out(T // 2 - 1)
            for i in range(2):
                sp.wait_ge(out_stored[i], 16 * (T // 2))

        @block.gpsimd
        def _(pool):
            pool.memset(ident[:, :], 0.0).then_inc(const_step, 1)
            pool.wait_ge(const_step, 1)
            pool.affine_select(out=ident[:, :], in_=ident[:, :], compare_op=ALU.not_equal, fill=1.0,
                               base=0, pattern=[[-1, P]], channel_multiplier=1).then_inc(const_ready, 1)
            pool.wait_ge(const_ready, 1)

            POOL_STEPS = NC + 5

            def prepare_mask(t, c):
                cols = slice(c * CHUNK, (c + 1) * CHUNK)
                if c == 0:
                    wait_apart(pool, adj_loaded, 16 * t + 16)
                pool.tensor_scalar(landing[:, cols], landing[:, cols], -1.0, None, ALU.add
                                   ).then_inc(pool_step, 1)

            def mask_diagonal(t):
                base = POOL_STEPS * t + NC
                here = bass.ds(t * P, P)
                pool.wait_ge(pool_step, base)
                pool.tensor_copy(diag[:, :], mask[:, 0, here]).then_inc(pool_step, 1)
                wait_apart(pool, pool_step, base + 1)
                pool.tensor_scalar(diag_pos[:, :], diag[:, :], 0.0, IDENTITY_BIAS / MASK_VAL,
                                   ALU.max, ALU.add).then_inc(pool_step, 1)
                pool.wait_ge(pool_step, base + 2)
                pool.tensor_tensor(diag_pos[:, :], diag_pos[:, :], ident[:, :], ALU.mult
                                   ).then_inc(pool_step, 1)
                pool.affine_select(out=diag[:, :], in_=diag[:, :], compare_op=ALU.not_equal, fill=0.0,
                                   base=0, pattern=[[-1, P]], channel_multiplier=1).then_inc(pool_step, 1)
                wait_apart(pool, pool_step, base + 4)
                pool.tensor_tensor(mask[:, 0, here], diag[:, :], diag_pos[:, :], ALU.add
                                   ).then_inc(pool_step, 1)

            def write_mask(t, c):
                if c == 0:
                    wait_apart(pool, pool_step, POOL_STEPS * (t + 1))
                cols = slice(c * CHUNK, (c + 1) * CHUNK)
                pool.tensor_scalar(addmask[:, cols], landing[:, cols], MASK_VAL, None, ALU.mult
                                   ).then_inc(mask_ready, 1)

            for c in range(NC):
                prepare_mask(0, c)
            mask_diagonal(0)
            for c in range(NC):
                write_mask(0, c)

            with pool.Fori(0, T - 1) as t:
                for c in range(NC):
                    prepare_mask(t + 1, c)
                mask_diagonal(t + 1)
                for c in range(NC):
                    wait_apart(pool, masked_ready, (t * H + H - 1) * NC + c + 1)
                    write_mask(t + 1, c)

        @block.tensor
        def _(pe):
            def make_xT(t):
                bank = bank_of(Q_HEADS[0], "queries")
                pe.wait_ge(xtile_loaded, 16 * t + 16)
                for c in range(DC):
                    mm = pe.transpose(bank[:, c * P:(c + 1) * P], x_tile[:, c * P:(c + 1) * P], ident[:, :])
                mm.then_inc(xT_made, 1)

            def make_q(t, part):
                bank = bank_of(Q_HEADS[1 + part], "queries")
                pe.wait_ge(xT_ready, t + 1)
                for j in range(HH // 2):
                    h = part * HH + 2 * j
                    for c in range(DC):
                        mm = pe.matmul(bank[:, j * P:(j + 1) * P],
                                       wq[:, c, h:h + 2, :].rearrange("p h k -> p (h k)"),
                                       xT_tile[:, c, :], start=(c == 0), stop=(c == DC - 1),
                                       skip_group_check=True)
                mm.then_inc(q_made, 1)

            pe.wait_ge(const_ready, 1)
            for n in range(DC * T // BS):
                if n < 8 and n % 2 == 0:
                    pe.wait_ge(x_loaded[n // 2], 16)
                if n >= 8:
                    pe.wait_ge(xT_emptied, n - 7)
                for b in range(BS):
                    blk = n * BS + b
                    mm = pe.transpose(banks[:, n % 8, b * P:(b + 1) * P],
                                      x_all[:, blk % T, (blk // T) * P:(blk // T + 1) * P], ident[:, :])
                mm.then_inc(xT_filled, 1)

            pe.wait_ge(xT_emptied, DC * T // BS)
            pe.wait_ge(wq_loaded, 16 * DC)
            make_xT(0)
            make_q(0, 0)
            make_q(0, 1)
            pe.wait_ge(q_lo_ready, 2)

            pe.wait_ge(wkv_loaded, 16 * 2 * DC)
            n = 0
            for j in range(H // 2):
                for m in range(NS):
                    if n >= 8:
                        pe.wait_ge(kv_lo, n - 7)
                    for c in range(DC):
                        mm = pe.matmul(banks[:, n % 8, :],
                                       wk[:, c, 2 * j:2 * j + 2, :].rearrange("p h k -> p (h k)"),
                                       xT_all[:, c, m * SUB:(m + 1) * SUB],
                                       start=(c == 0), stop=(c == DC - 1))
                    mm.then_inc(kv_filled, 1)
                    n += 1
            for t in range(T):
                pe.wait_ge(kv_lo, n - 7)
                for c in range(DC):
                    mm = pe.matmul(banks[:, n % 8, :], xT_all[:, c, t * P:(t + 1) * P],
                                   wv[:, c].rearrange("p h k -> p (h k)"),
                                   start=(c == 0), stop=(c == DC - 1))
                mm.then_inc(kv_filled, 1)
                n += 1
            pe.wait_ge(kv_lo, n)
            for i in range(2):
                pe.wait_ge(k_spread[i], 64 * (H // 4))

            def scores(g, h, c, t):
                if c == 0 and h % HH == 0:
                    pe.wait_ge(q_spread[h // HH], 96 * (t + 1))
                if not (isinstance(g, int) and g == 0 and c < 2):
                    pe.wait_ge(masked_ready, g * NC + c - 1)
                for part, q in enumerate((q_hi, q_lo)):
                    for b in range(CHUNK // SUB):
                        mm = pe.matmul(score_ps[c % 2][:, b, :], q[:, h, :],
                                       kstack[:, h, c * CHUNK + b * SUB:c * CHUNK + (b + 1) * SUB],
                                       start=(part == 0), stop=(part == 1), skip_group_check=True)
                mm.then_inc(scores_ready, 1)

            def turn(g, h, s):
                if s % 2 == 0:
                    pe.wait_ge(exp_ready, g * NC + s // 2 + 1)
                bank = bank_of(h, s)
                for b in range(BS):
                    m = s * BS + b
                    mm = pe.transpose(bank[:, b * P:(b + 1) * P], prob[:, h % 2, m * P:(m + 1) * P],
                                      ident[:, :])
                mm.then_inc(transposed, 1)

            def values(g, h, s):
                pe.wait_ge(lo_ready, g * NS + s + 1)
                for b in range(BS):
                    m = s * BS + b
                    mm = pe.matmul(av_ps, vstack[:, h, m, :],
                                   probT[:, s % NPT, b].rearrange("p s q -> p (s q)"),
                                   start=(m == 0), stop=(m == T - 1))
                mm.then_inc(av_done, 1)

            def project(g, h):
                pe.wait_ge(head_ready, g + 1)
                mm = pe.matmul(bank_of((h + 1) % H, "project")[:, 0:D], head_out[:, :], wreg[:, h, :],
                               start=True, stop=True)
                mm.then_inc(projected, 1)

            for c in range(NC):
                scores(0, 0, c, 0)
            pe.wait_ge(wo_loaded, 32)

            def tile(t, first=False, last=False):
                for h in range(H):
                    g = t * H + h
                    ahead = not (last and h == H - 1)
                    nh, nt = (h + 1, t) if h < H - 1 else (0, t + 1)
                    before = not (first and h == 0)
                    ph = (h - 1) % H
                    late = h in Q_HEADS
                    if first and h == 0:
                        scores(g + 1, nh, 0, nt)
                    turn(g, h, 0)
                    if before:
                        values(g - 1, ph, 6)
                    turn(g, h, 1)
                    if before:
                        values(g - 1, ph, 7)
                    if ahead:
                        scores(g + 1, nh, 1, nt)
                    turn(g, h, 2)
                    pe.wait_ge(lo_ready, g * NS + 1)
                    turn(g, h, 3)
                    if before:
                        pe.wait_ge(parts_ready, g)
                    values(g, h, 0)
                    values(g, h, 1)
                    if before:
                        project(g - 1, ph)
                    if ahead:
                        scores(g + 1, nh, 2, nt)
                    pe.wait_ge(lo_ready, g * NS + 3)
                    if late:
                        if not last:
                            if h == Q_HEADS[0]:
                                make_xT(t + 1)
                            else:
                                make_q(t + 1, Q_HEADS.index(h) - 1)
                        if h == Q_HEADS[0]:
                            values(g, h, 2)
                        pe.wait_ge(lo_ready, g * NS + 4)
                    turn(g, h, 4)
                    if h != Q_HEADS[0]:
                        values(g, h, 2)
                    if late:
                        pe.wait_ge(y_added, g)
                    else:
                        pe.wait_ge(lo_ready, g * NS + 4)
                    turn(g, h, 5)
                    if ahead:
                        scores(g + 1, nh, 3, nt)
                    values(g, h, 3)
                    if not late:
                        if before:
                            pe.wait_ge(y_added, g)
                    elif not last:
                        if h == Q_HEADS[0]:
                            pe.wait_ge(xT_ready, t + 2)
                        else:
                            pe.wait_ge(q_lo_ready, 2 * t + 2 + Q_HEADS.index(h))
                    turn(g, h, 6)
                    values(g, h, 4)
                    turn(g, h, 7)
                    if not (last and h >= H - 2):
                        h2, t2 = (h + 2, t) if h < H - 2 else (h + 2 - H, t + 1)
                        scores(g + 2, h2, 0, t2)
                    values(g, h, 5)

            tile(0, first=True)
            with pe.Fori(1, T - 1) as t:
                tile(t)
            tile(T - 1, last=True)
            pe.wait_ge(masked_ready, T * H * NC)
            pe.wait_ge(w1_loaded, 64)
            for i in range(2):
                for c in range(DC):
                    for o in range(2):
                        mm = pe.transpose(banks[:, i, c * D + o * P:c * D + (o + 1) * P],
                                          w_raw[i][:, o, c * P:(c + 1) * P], ident[:, :])
                mm.then_inc(wT_made, 1)
            values(T * H - 1, H - 1, 6)
            values(T * H - 1, H - 1, 7)
            project(T * H - 1, H - 1)

            pe.wait_ge(wT_ready, 2)
            pe.wait_ge(y_added, T * H)
            for t in range(T + 1):
                if t < T:
                    pe.wait_ge(normed, t + 1)
                    if t >= 2:
                        pe.wait_ge(hT_ready, t - 1)
                    for c in range(DC):
                        mm = pe.transpose(banks[:, 2 + t % 2, c * P:(c + 1) * P],
                                          h32[:, t, c * P:(c + 1) * P], ident[:, :])
                    mm.then_inc(hT_made, 1)
                if t >= 1:
                    u = t - 1
                    pe.wait_ge(hT_ready, u + 1)
                    if u >= 4:
                        pe.wait_ge(g_lo_ready, u - 3)
                    for c in range(DC):
                        mm = pe.matmul(banks[:, 4 + u % 4, :], hT[u % 2][:, c, :], wT[:, c, :],
                                       start=(c == 0), stop=(c == DC - 1))
                    mm.then_inc(linear_made, 1)

            def turn_adj(t, i, k):
                if k == 0:
                    if isinstance(t, int) and t < 2:
                        pe.wait_ge(deg_part_ready, NC * (t + 1))
                    else:
                        pe.wait_ge(adj16_ready, t - 1)
                if not (isinstance(t, int) and t == 0):
                    if k == 0:
                        pe.wait_ge(adjT_by_act, t)
                    else:
                        pe.wait_ge(adjT_by_dve, 3 * t + k - 3)
                bank = banks[:, k, :].bitcast(F16)
                for b in range(8):
                    m = 8 * k + b
                    mm = pe.transpose(bank[:, b * P:(b + 1) * P], adj16[i][:, m * P:(m + 1) * P],
                                      ident16[:, :])
                mm.then_inc(adjT_made, 1)

            def aggregate(t, i, k):
                if k == 0:
                    pe.wait_ge(adjT_by_act, t + 1)
                else:
                    pe.wait_ge(adjT_by_dve, 3 * t + k)
                for b in range(8):
                    m = 8 * k + b
                    mm = pe.matmul(banks[:, 4 + i, :], adjT[i][:, m * P:(m + 1) * P],
                                   gsplit[:, m].rearrange("p s d -> p (s d)"),
                                   start=(m == 0), stop=(m == T - 1))
                if k == 3:
                    mm.then_inc(agg_done, 1)

            pe.wait_ge(hT_ready, T)
            pe.wait_ge(ident16_ready, 1)
            for k in range(4):
                turn_adj(0, 0, k)
            pe.wait_ge(g_lo_ready, T)

            def pair(t2, first=False, last=False):
                for i in range(2):
                    t = 2 * t2 + i
                    for k in range(4):
                        if not (last and i == 1):
                            turn_adj(t + 1, 1 - i, k)
                        if k == 0 and not first:
                            pe.wait_ge(neigh_ready, t - 1)
                        aggregate(t, i, k)

            pair(0, first=True)
            with pe.Fori(1, T // 2 - 1) as t2:
                pair(t2)
            pair(T // 2 - 1, last=True)

        @block.scalar
        def _(act):
            for n in range(DC * T // BS):
                act.wait_ge(xT_filled, n + 1)
                blk = n * BS
                act.activation(xT_all[:, blk // T, (blk % T) * P:(blk % T + BS) * P], banks[:, n % 8, :],
                               ACT.Copy).then_inc(xT_emptied, 1)
            def copy_xT(t):
                act.wait_ge(xT_made, t + 1)
                act.activation(xT_tile[:, :, :].rearrange("p c q -> p (c q)"),
                               bank_of(Q_HEADS[0], "queries")[:, 0:D], ACT.Copy).then_inc(xT_ready, 1)

            def high_q(t, part):
                act.wait_ge(q_made, 2 * t + part + 1)
                act.activation(q_hi[:, part * HH:(part + 1) * HH:2, :],
                               bank_of(Q_HEADS[1 + part], "queries")[:, 0:2 * P].rearrange(
                                   "p (j q) -> p j q", j=2), ACT.Copy, scale=SCALE).then_inc(q_hi_ready, 1)

            copy_xT(0)
            high_q(0, 0)
            high_q(0, 1)
            n = 0
            for j in range(H // 2):
                for m in range(NS):
                    act.wait_ge(kv_filled, n + 1)
                    if m == 0 and j >= 2:
                        act.wait_ge(k_spread[j % 2], 64 * (j // 2))
                    act.activation(k_pair[:, j % 2, 0, m * SUB:(m + 1) * SUB], banks[:, n % 8, :], ACT.Copy
                                   ).then_inc(kv_hi, 1)
                    n += 1
            for i in range(2):
                act.wait_ge(k_spread[i], 64 * (H // 4))
            for t in range(T):
                act.wait_ge(kv_filled, n + 1)
                act.activation(vstack[:, :, t, 0:KD], banks[:, n % 8, :].rearrange("p (h k) -> p h k", h=H),
                               ACT.Copy).then_inc(kv_hi, 1)
                n += 1

            def exps(g, h, c):
                if c == 0:
                    act.wait_ge(neg_max_ready, g + 1)
                cols = prob[:, h % 2, c * CHUNK:(c + 1) * CHUNK]
                act.activation(cols, cols, ACT.Exp, bias=neg_max[:, h % 2:h % 2 + 1],
                               accum_out=chunk_sum[:, h % 2, c:c + 1]).then_inc(exp_ready, 1)

            def high(g, h, s):
                act.wait_ge(transposed, g * NS + s + 1)
                act.activation(probT[:, s % NPT, :, 0, :], bank_of(h, s).rearrange("p (b q) -> p b q", b=BS),
                               ACT.Copy).then_inc(hi_ready, 1)

            def take_parts(g):
                act.wait_ge(av_done, g * NS + NS)
                act.activation(head_parts[:, :, :].rearrange("p s q -> p (s q)"), av_ps, ACT.Copy
                               ).then_inc(parts_ready, 1)

            exps(0, 0, 0)

            def tile(t, first=False, last=False):
                for h in range(H):
                    g = t * H + h
                    high(g, h, 0)
                    exps(g, h, 1)
                    high(g, h, 1)
                    if not (first and h == 0):
                        take_parts(g - 1)
                    high(g, h, 2)
                    exps(g, h, 2)
                    high(g, h, 3)
                    exps(g, h, 3)
                    if h in Q_HEADS and not last:
                        if h == Q_HEADS[0]:
                            copy_xT(t + 1)
                        else:
                            high_q(t + 1, Q_HEADS.index(h) - 1)
                    high(g, h, 4)
                    high(g, h, 5)
                    high(g, h, 6)
                    if not (last and h == H - 1):
                        exps(g + 1, h + 1, 0)
                    high(g, h, 7)

            tile(0, first=True)
            with act.Fori(1, T - 1) as t:
                tile(t)
            tile(T - 1, last=True)
            for i in range(2):
                act.wait_ge(wT_made, i + 1)
                act.activation(wT[:, :, i * D:(i + 1) * D],
                               banks[:, i, :].rearrange("p (c o) -> p c o", c=DC), ACT.Copy
                               ).then_inc(wT_ready, 1)
            take_parts(T * H - 1)

            def deviations(first, last, kept):
                act.wait_ge(mv_kept, kept)
                act.activation(std_all[:, first:last], mean_var[:, first:last, 1], ACT.Sqrt, bias=eps_col
                               ).then_inc(std_ready, 1)

            def convert_chunk(i, c):
                if c == 0:
                    act.wait_ge(adj1_loaded[i], 16)
                cols = slice(c * CHUNK, (c + 1) * CHUNK)
                act.activation(adj16[i][:, cols], mask[:, i, cols], ACT.Copy,
                               accum_out=deg_part[i][:, c:c + 1]).then_inc(deg_part_ready, 1)

            act.wait_ge(eps_ready, 1)
            deviations(0, T - 1, T - 1)
            for t in range(T + 1):
                if t < T:
                    act.wait_ge(hT_made, t + 1)
                    if t >= 2:
                        act.wait_ge(linear_made, t - 1)
                    act.activation(hT[t % 2].rearrange("p c q -> p (c q)"), banks[:, 2 + t % 2, 0:D],
                                   ACT.Copy).then_inc(hT_ready, 1)
                if t == T // 2:
                    deviations(T - 1, T, T)
                if t >= 1:
                    act.wait_ge(linear_made, t)
                    act.activation(gsplit[:, t - 1, 0, :], banks[:, 4 + (t - 1) % 4, D:2 * D], ACT.Copy
                                   ).then_inc(g_hi_ready, 1)
                if t % 3 == 0 and 0 < t <= 6 * NC:
                    convert_chunk((t // 3 - 1) // NC, (t // 3 - 1) % NC)

            def convert(t, i, t2):
                act.wait_ge(adj1_loaded[i], 16 * t2 + 16)
                act.wait_ge(adjT_made, 4 * t - 4)
                act.wait_ge(inv_deg_ready, 2 * t - 2)
                act.activation(adj16[i], mask[:, i, :], ACT.Copy, accum_out=deg_raw[i]
                               ).then_inc(adj16_ready, 1)

            def empty_adj(t, i, k):
                act.wait_ge(adjT_made, 4 * t + k + 1)
                if not (isinstance(t, int) and t < 2):
                    act.wait_ge(agg_done, t - 1)
                act.activation(adjT[i][:, 8 * k * P:8 * (k + 1) * P], banks[:, k, :].bitcast(F16), ACT.Copy
                               ).then_inc(adjT_by_act, 1)

            def scale_low(t, i):
                act.wait_ge(agg_done, t + 1)
                act.wait_ge(inv_deg_ready, 2 * t + 2)
                act.activation(agg_lo[i], banks[:, 4 + i, D:2 * D], ACT.Copy, scale=inv_deg[i]
                               ).then_inc(agg_lo_ready, 1)

            def deviation(t, i):
                act.wait_ge(z_step, 4 * t + 4)
                act.activation(std1[i], mean_var1[i][:, 1:2], ACT.Sqrt, bias=eps_col).then_inc(std1_ready, 1)

            empty_adj(0, 0, 0)

            def pair(t2, first=False, last=False):
                for i in range(2):
                    t = 2 * t2 + i
                    more = not (last and i == 1)
                    before = not (first and i == 0)
                    if before:
                        scale_low(t - 1, 1 - i)
                    if more:
                        empty_adj(t + 1, 1 - i, 0)
                    if not last:
                        convert(t + 2, i, t2 + 1)
                    if before:
                        deviation(t - 1, 1 - i)

            pair(0, first=True)
            with act.Fori(1, T // 2 - 1) as t2:
                pair(t2)
            pair(T // 2 - 1, last=True)
            scale_low(T - 1, 1)
            deviation(T - 1, 1)

        @block.vector
        def _(dve):
            def low_q(t, part):
                dve.wait_ge(q_hi_ready, 2 * t + part + 1)
                even = slice(part * HH, (part + 1) * HH, 2)
                dve.scalar_tensor_tensor(out=q_lo[:, even, :],
                                         in0=bank_of(Q_HEADS[1 + part], "queries")[:, 0:2 * P].rearrange(
                                             "p (j q) -> p j q", j=2), scalar=SCALE, in1=q_hi[:, even, :],
                                         op0=ALU.mult, op1=ALU.subtract).then_inc(q_lo_ready, 1)

            low_q(0, 0)
            low_q(0, 1)
            n = 0
            for j in range(H // 2):
                for m in range(NS):
                    dve.wait_ge(kv_hi, n + 1)
                    cols = slice(m * SUB, (m + 1) * SUB)
                    dve.tensor_tensor(k_pair[:, j % 2, 1, cols], banks[:, n % 8, :], k_pair[:, j % 2, 0, cols],
                                      ALU.subtract).then_inc(kv_lo, 1)
                    n += 1
            for t in range(T):
                dve.wait_ge(kv_hi, n + 1)
                dve.tensor_tensor(vstack[:, :, t, KD:P], banks[:, n % 8, :].rearrange("p (h k) -> p h k", h=H),
                                  vstack[:, :, t, 0:KD], ALU.subtract).then_inc(kv_lo, 1)
                n += 1

            def y_stats(t):
                dve.wait_ge(y_added, t * H + H)
                dve.bn_stats(y_stat[:, :], y_tile[:, :]).then_inc(stats_ready, 1)

            def y_aggr(t):
                wait_apart(dve, stats_ready, t + 1)
                dve.bn_aggr(y_mean_var[:, :], y_stat[:, :]).then_inc(mv_ready, 1)

            def y_keep(t):
                wait_apart(dve, mv_ready, t + 1)
                dve.tensor_copy(mean_var[:, bass.ds(t, 1), :].rearrange("p t s -> p (t s)"), y_mean_var[:, :]
                                ).then_inc(mv_kept, 1)

            def add_mask(g, h, c, t):
                if h == 0:
                    wait_apart(dve, mask_ready, t * NC + c + 1)
                wait_apart(dve, scores_ready, g * NC + c + 1)
                cols = slice(c * CHUNK, (c + 1) * CHUNK)
                dve.tensor_tensor_reduce(prob[:, h % 2, cols],
                                         score_ps[c % 2].rearrange("p b n -> p (b n)"), addmask[:, cols],
                                         1.0, LOWEST, ALU.add, ALU.max,
                                         chunk_max[:, h % 2, c:c + 1]).then_inc(masked_ready, 1)

            def max_of_row(g, h):
                dve.wait_ge(masked_ready, g * NC + NC)
                dve.tensor_reduce(neg_max[:, h % 2:h % 2 + 1], chunk_max[:, h % 2, :], AX.X, ALU.max,
                                  negate=True).then_inc(neg_max_ready, 1)

            def low(g, h, s):
                dve.wait_ge(hi_ready, g * NS + s + 1)
                dve.tensor_tensor(probT[:, s % NPT, :, 1, :], bank_of(h, s).rearrange("p (b q) -> p b q", b=BS),
                                  probT[:, s % NPT, :, 0, :], ALU.subtract).then_inc(lo_ready, 1)

            def add_parts(g):
                dve.wait_ge(parts_ready, g + 1)
                dve.tensor_tensor(head_out[:, :], head_parts[:, 0, :], head_parts[:, 1, :], ALU.add
                                  ).then_inc(head_ready, 1)

            def sum_row(g, h):
                dve.wait_ge(exp_ready, g * NC + NC)
                dve.tensor_reduce(row_sum[:, :], chunk_sum[:, h % 2, :], AX.X, ALU.add).then_inc(sum_ready, 1)

            def invert_sum(g):
                dve.wait_ge(sum_ready, g + 1)
                dve.reciprocal(inv_sum[:, :], row_sum[:, :]).then_inc(inv_ready, 1)

            def add_head(g, h, t):
                dve.wait_ge(projected, g + 1)
                dve.wait_ge(inv_ready, g + 1)
                if h > 0:
                    dve.wait_ge(y_added, g)
                else:
                    dve.wait_ge(xtile_loaded, 16 * t + 16)
                    if not (isinstance(t, int) and t == 0):
                        dve.wait_ge(y_stored, 16 * t)
                dve.scalar_tensor_tensor(out=y_tile[:, :], in0=bank_of((h + 1) % H, "project")[:, 0:D],
                                         scalar=inv_sum[:, 0:1],
                                         in1=x_tile[:, :] if h == 0 else y_tile[:, :],
                                         op0=ALU.mult, op1=ALU.add).then_inc(y_added, 1)

            for c in range(NC):
                add_mask(0, 0, c, 0)
            max_of_row(0, 0)

            def tile(t, first=False, last=False):
                for h in range(H):
                    g = t * H + h
                    ahead = not (last and h == H - 1)
                    nh, nt = (h + 1, t) if h < H - 1 else (0, t + 1)
                    if ahead:
                        add_mask(g + 1, nh, 0, nt)
                    low(g, h, 0)
                    low(g, h, 1)
                    if not (first and h == 0):
                        add_parts(g - 1)
                    if not first and h == 1:
                        y_keep(t - 1)
                    if ahead:
                        add_mask(g + 1, nh, 1, nt)
                    low(g, h, 2)
                    low(g, h, 3)
                    if h in Q_HEADS:
                        add_head(g - 1, (h - 1) % H, t)
                    if ahead:
                        add_mask(g + 1, nh, 2, nt)
                    if h not in Q_HEADS and not (first and h == 0):
                        add_head(g - 1, (h - 1) % H, t)
                    sum_row(g, h)
                    if h in Q_HEADS[1:] and not last:
                        low_q(t + 1, Q_HEADS.index(h) - 1)
                    low(g, h, 4)
                    invert_sum(g)
                    if ahead:
                        add_mask(g + 1, nh, 3, nt)
                        max_of_row(g + 1, nh)
                    low(g, h, 5)
                    low(g, h, 6)
                    if not first and h == 0:
                        y_stats(t - 1)
                    low(g, h, 7)
                    if not first and h == 0:
                        y_aggr(t - 1)

            tile(0, first=True)
            with dve.Fori(1, T - 1) as t:
                tile(t)
            tile(T - 1, last=True)
            dve.memset(eps_col, LN_EPS).then_inc(eps_ready, 1)
            dve.tensor_copy(ident16, ident[:, :]).then_inc(ident16_ready, 1)
            dve.wait_ge(w1_loaded, 64)
            dve.tensor_tensor(bias_sum, bias_bc[0], bias_bc[1], ALU.add).then_inc(bias_ready, 1)
            add_parts(T * H - 1)
            add_head(T * H - 1, H - 1, T - 1)

            def invert_deviations(first, last, count):
                dve.wait_ge(std_ready, count)
                dve.reciprocal(inv_std_all[:, first:last], std_all[:, first:last]).then_inc(inv_std_ready, 1)
                dve.wait_ge(inv_std_ready, count)

            def normalise_y(t):
                if t == T - 1:
                    dve.wait_ge(y_last_loaded, 16)
                elif t % (T // 4) == 0:
                    dve.wait_ge(y_loaded[t // (T // 4)], 16)
                dve.tensor_scalar(h32[:, t, :], h32[:, t, :], mean_var[:, t, 0:1],
                                  inv_std_all[:, t:t + 1], ALU.subtract, ALU.mult).then_inc(normed, 1)

            def take_linear(u):
                dve.wait_ge(g_hi_ready, u + 1)
                dve.tensor_tensor(self_term[:, u, :], banks[:, 4 + u % 4, 0:D], bias_sum, ALU.add
                                  ).then_inc(self_ready, 1)
                dve.tensor_tensor(gsplit[:, u, 1, :], banks[:, 4 + u % 4, D:2 * D], gsplit[:, u, 0, :],
                                  ALU.subtract).then_inc(g_lo_ready, 1)

            y_stats(T - 1)
            y_aggr(T - 1)
            dve.wait_ge(bias_ready, 1)
            invert_deviations(0, T - 1, 1)
            y_keep(T - 1)
            AHEAD = 3
            for t in range(T + AHEAD):
                if t == T - 1:
                    invert_deviations(T - 1, T, 2)
                if t < T:
                    normalise_y(t)
                if t >= AHEAD:
                    take_linear(t - AHEAD)

            for i in range(2):
                dve.wait_ge(deg_part_ready, NC * (i + 1))
                dve.tensor_reduce(deg_raw[i], deg_part[i], AX.X, ALU.add).then_inc(deg_raw_ready, 1)
                dve.wait_ge(deg_raw_ready, i + 1)

            def degree(t, i):
                if not (isinstance(t, int) and t < 2):
                    dve.wait_ge(adj16_ready, t - 1)
                    dve.wait_ge(neigh_ready, t - 1)
                dve.tensor_scalar(deg[i], deg_raw[i], DEG_EPS, None, ALU.add).then_inc(inv_deg_ready, 1)
                dve.wait_ge(inv_deg_ready, 2 * t + 1)
                dve.reciprocal(inv_deg[i], deg[i]).then_inc(inv_deg_ready, 1)

            def empty_adj(t, i, k):
                dve.wait_ge(adjT_made, 4 * t + k + 1)
                if not (isinstance(t, int) and t < 2):
                    dve.wait_ge(agg_done, t - 1)
                dve.tensor_copy(adjT[i][:, 8 * k * P:8 * (k + 1) * P], banks[:, k, :].bitcast(F16)
                                ).then_inc(adjT_by_dve, 1)

            def neighbours(t, i):
                dve.wait_ge(agg_lo_ready, t + 1)
                dve.scalar_tensor_tensor(out=neigh[i], in0=banks[:, 4 + i, 0:D], scalar=inv_deg[i],
                                         in1=agg_lo[i], op0=ALU.mult, op1=ALU.add).then_inc(neigh_ready, 1)

            def add_and_relu(t, i):
                dve.wait_ge(neigh_ready, t + 1)
                if isinstance(t, int) and t == 0:
                    dve.wait_ge(self_ready, T)
                dve.tensor_tensor(z[i], neigh[i], self_term[:, t, :], ALU.add).then_inc(z_step, 1)
                dve.wait_ge(z_step, 4 * t + 1)
                dve.scalar_tensor_tensor(out=z[i], in0=z[i], scalar=0.0, in1=h32[:, t, :],
                                         op0=ALU.max, op1=ALU.add).then_inc(z_step, 1)
                dve.wait_ge(z_step, 4 * t + 2)
                dve.bn_stats(stats1[i], z[i]).then_inc(z_step, 1)
                wait_apart(dve, z_step, 4 * t + 3)
                dve.bn_aggr(mean_var1[i], stats1[i]).then_inc(z_step, 1)

            def normalise(t, i, stored):
                dve.wait_ge(std1_ready, t + 1)
                dve.reciprocal(inv_std1[i], std1[i]).then_inc(inv_std_ready, 1)
                dve.wait_ge(inv_std_ready, t + 3)
                if not (isinstance(stored, int) and stored <= 0):
                    dve.wait_ge(out_stored[i], 16 * stored)
                dve.tensor_scalar(o_tile[i], z[i], mean_var1[i][:, 0:1], inv_std1[i],
                                  ALU.subtract, ALU.mult).then_inc(out_ready, 1)

            degree(0, 0)
            for k in range(1, 4):
                empty_adj(0, 0, k)

            def pair(t2, first=False, last=False):
                for i in range(2):
                    t = 2 * t2 + i
                    more = not (last and i == 1)
                    if not (first and i == 0):
                        neighbours(t - 1, 1 - i)
                    if more:
                        degree(t + 1, 1 - i)
                        empty_adj(t + 1, 1 - i, 1)
                        empty_adj(t + 1, 1 - i, 2)
                    if not (first and i == 0):
                        add_and_relu(t - 1, 1 - i)
                    if more:
                        empty_adj(t + 1, 1 - i, 3)
                    if not (first and i == 0):
                        normalise(t - 1, 1 - i, t2 - 1 + i)

            pair(0, first=True)
            with dve.Fori(1, T // 2 - 1) as t2:
                pair(t2)
            pair(T // 2 - 1, last=True)
            neighbours(T - 1, 1)
            add_and_relu(T - 1, 1)
            normalise(T - 1, 1, T // 2 - 1)


_INS = ['x', 'adj', 'L0_gnn_Wks', 'L0_gnn_Wqs', 'L0_gnn_Wvs', 'L0_gnn_Wo',
        'L1_gnn_W_neigh', 'L1_gnn_b_neigh', 'L1_gnn_W_self', 'L1_gnn_b_self']
_OUTS = [((4096, 256), 'float32')]


def kernel(**inputs):
    import numpy as _np
    import concourse.bacc as _bacc
    from concourse import mybir as _mybir
    from concourse.bass_utils import run_bass_kernel_spmd as _run

    nc = _bacc.Bacc("TRN2", target_bir_lowering=False, num_devices=1, dynamic_dma_scratch_size=1024)
    arrays, args = {}, []
    for name in _INS:
        a = _np.ascontiguousarray(inputs[name])
        arrays[f"in_{name}_dram"] = a
        args.append(nc.dram_tensor(f"in_{name}_dram", a.shape, _mybir.dt.from_np(a.dtype), kind="ExternalInput").ap())
    for i, (shape, dtype) in enumerate(_OUTS):
        dt = _mybir.dt.from_np(_np.dtype(dtype))
        args.append(nc.dram_tensor(f"out_{i}_dram", shape, dt, kind="ExternalOutput").ap())
    gnn_two_layers(nc, *args)
    r = _run(nc, [arrays], core_ids=[0])
    got = tuple(r.results[0][f"out_{i}_dram"] for i in range(len(_OUTS)))
    return got[0]
```
